# Optimizing a Trainium2 kernel written in Bass

```python
import numpy as np
import jax
import jax.numpy as jnp

def _softmax(x, axis=-1):
    return jax.nn.softmax(x, axis=axis)

def _gelu(x):
    return jax.nn.gelu(x, approximate=True)

def _silu(x):
    return jax.nn.silu(x)

def _sigmoid(x):
    return jax.nn.sigmoid(x)

def _layernorm(x, axis=-1, eps=1e-05):
    m = jnp.mean(x, axis=axis, keepdims=True)
    v = jnp.var(x, axis=axis, keepdims=True)
    return (x - m) / jnp.sqrt(v + eps)

def _scatter_add(tgt, idx, src, axis=0):
    return tgt.at[idx].add(src)

def _segment_sum(src, seg, n):
    return jax.ops.segment_sum(src, seg, n)
kernel_name = 'mk_cond_resid_d1_seqx_r2_de61b8'

def setup_inputs(seed: int=0):
    np.random.seed(seed)
    _w = jnp.asarray

    def _rec_inputs():
        import jax
        import jax.numpy as jnp
        _rk = jax.random.key(seed)
        x = -0.0002928 + 1 * jax.random.normal(jax.random.fold_in(_rk, 1), (8, 512, 512), jnp.float32)
        _lenS = 512 - jax.random.randint(jax.random.fold_in(_rk, 7), (8,), 0, max(1, 512 // 4) + 1, jnp.int32)
        _lenS2 = 512 - jax.random.randint(jax.random.fold_in(_rk, 8), (8,), 0, max(1, 512 // 4) + 1, jnp.int32)
        cond_64 = -0.0184271 + 1.00439 * jax.random.normal(jax.random.fold_in(_rk, 12), (8, 64), jnp.float32)
        _validS = jnp.arange(512)[None, :] < _lenS[:, None]
        _validS2 = jnp.arange(512)[None, :] < _lenS2[:, None]
        _causal = jnp.tril(jnp.ones((512, 512), dtype=bool))
        mask_BxS_bf1 = jnp.ones((8, 512), dtype=bool)
        return (x, cond_64, mask_BxS_bf1)
    x, cond_64, mask_BxS_bf1 = _rec_inputs()

    def _L0_cond_setup():
        import jax, jax.numpy as jnp
        import numpy as np
        DIM = 512
        HEADS = 16
        DIM_HEAD = 64
        SCALE = 8.0

        def ln(x, g, eps=1e-05):
            mean = x.mean(axis=-1, keepdims=True)
            var = ((x - mean) ** 2).mean(axis=-1, keepdims=True)
            return (x - mean) * jax.lax.rsqrt(var + eps) * g

        def l2norm(t):
            n = jnp.maximum(jnp.linalg.norm(t, axis=-1, keepdims=True), 1e-12)
            return t / n

        def rel_pos_bias(n, w0, b0, g0, w1, b1, g1, w2, b2, dtype):
            pos = jnp.arange(-n + 1, n, dtype=dtype)[:, None]
            h = jax.nn.silu(ln(pos @ w0 + b0, g0))
            h = jax.nn.silu(ln(h @ w1 + b1, g1))
            h = h @ w2 + b2
            i = jnp.arange(n)
            idx = i[:, None] - i[None, :] + n - 1
            bias = h[idx]
            return jnp.transpose(bias, (2, 0, 1))
        key = jax.random.key(seed)
        ks = jax.random.split(key, 16)
        b, n = (2, 1024)
        inner = HEADS * DIM_HEAD
        s = 0.02
        return {'x': jax.random.normal(ks[0], (b, n, DIM), jnp.float32), 'mask': jnp.ones((b, n), dtype=bool), 'g_norm': jnp.ones((DIM,), jnp.float32), 'Wq': jax.random.normal(ks[1], (DIM, inner), jnp.float32) * s, 'Wkv': jax.random.normal(ks[2], (DIM, 2 * DIM_HEAD), jnp.float32) * s, 'q_scale': jnp.ones((DIM_HEAD,), jnp.float32), 'k_scale': jnp.ones((DIM_HEAD,), jnp.float32), 'null_kv': jax.random.normal(ks[3], (2, DIM_HEAD), jnp.float32), 'null_attn_bias': jax.random.normal(ks[4], (HEADS,), jnp.float32), 'w0': jax.random.normal(ks[5], (1, DIM), jnp.float32) * s, 'b0': jnp.zeros((DIM,), jnp.float32), 'g0': jnp.ones((DIM,), jnp.float32), 'w1': jax.random.normal(ks[6], (DIM, DIM), jnp.float32) * s, 'b1': jnp.zeros((DIM,), jnp.float32), 'g1': jnp.ones((DIM,), jnp.float32), 'w2': jax.random.normal(ks[7], (DIM, HEADS), jnp.float32) * s, 'b2': jnp.zeros((HEADS,), jnp.float32), 'Wout': jax.random.normal(ks[8], (inner, DIM), jnp.float32) * s, 'g_out': jnp.ones((DIM,), jnp.float32)}
    _L0_cond_all = _L0_cond_setup()
    _L0_cond_in = {k: v for k, v in _L0_cond_all.items() if k in ('g_norm', 'Wq', 'Wkv', 'q_scale', 'k_scale', 'null_attn_bias', 'w0', 'b0', 'g0', 'w1', 'b1', 'g1', 'w2', 'b2', 'Wout', 'g_out')}
    del _L0_cond_all
    return {'x': x, 'cond_64': cond_64, 'mask_BxS_bf1': mask_BxS_bf1, 'L0_cond_g_norm': _L0_cond_in['g_norm'], 'L0_cond_Wq': _L0_cond_in['Wq'], 'L0_cond_Wkv': _L0_cond_in['Wkv'], 'L0_cond_q_scale': _L0_cond_in['q_scale'], 'L0_cond_k_scale': _L0_cond_in['k_scale'], 'L0_cond_null_attn_bias': _L0_cond_in['null_attn_bias'], 'L0_cond_w0': _L0_cond_in['w0'], 'L0_cond_b0': _L0_cond_in['b0'], 'L0_cond_g0': _L0_cond_in['g0'], 'L0_cond_w1': _L0_cond_in['w1'], 'L0_cond_b1': _L0_cond_in['b1'], 'L0_cond_g1': _L0_cond_in['g1'], 'L0_cond_w2': _L0_cond_in['w2'], 'L0_cond_b2': _L0_cond_in['b2'], 'L0_cond_Wout': _L0_cond_in['Wout'], 'L0_cond_g_out': _L0_cond_in['g_out']}

def reference(x, cond_64, mask_BxS_bf1, L0_cond_g_norm, L0_cond_Wq, L0_cond_Wkv, L0_cond_q_scale, L0_cond_k_scale, L0_cond_null_attn_bias, L0_cond_w0, L0_cond_b0, L0_cond_g0, L0_cond_w1, L0_cond_b1, L0_cond_g1, L0_cond_w2, L0_cond_b2, L0_cond_Wout, L0_cond_g_out):
    import jax
    import jax.numpy as jnp

    def _L0_cond_ref(x, mask, g_norm, Wq, Wkv, q_scale, k_scale, null_kv, null_attn_bias, w0, b0, g0, w1, b1, g1, w2, b2, Wout, g_out):
        import jax, jax.numpy as jnp
        import numpy as np
        DIM = 512
        HEADS = 16
        DIM_HEAD = 64
        SCALE = 8.0

        def ln(x, g, eps=1e-05):
            mean = x.mean(axis=-1, keepdims=True)
            var = ((x - mean) ** 2).mean(axis=-1, keepdims=True)
            return (x - mean) * jax.lax.rsqrt(var + eps) * g

        def l2norm(t):
            n = jnp.maximum(jnp.linalg.norm(t, axis=-1, keepdims=True), 1e-12)
            return t / n

        def rel_pos_bias(n, w0, b0, g0, w1, b1, g1, w2, b2, dtype):
            pos = jnp.arange(-n + 1, n, dtype=dtype)[:, None]
            h = jax.nn.silu(ln(pos @ w0 + b0, g0))
            h = jax.nn.silu(ln(h @ w1 + b1, g1))
            h = h @ w2 + b2
            i = jnp.arange(n)
            idx = i[:, None] - i[None, :] + n - 1
            bias = h[idx]
            return jnp.transpose(bias, (2, 0, 1))
        b, n, _ = x.shape
        xn = ln(x, g_norm)
        q = (xn @ Wq).reshape(b, n, HEADS, DIM_HEAD).transpose(0, 2, 1, 3)
        kv = xn @ Wkv
        k, v = (kv[..., :DIM_HEAD], kv[..., DIM_HEAD:])
        nk = jnp.broadcast_to(null_kv[0], (b, 1, DIM_HEAD))
        nv = jnp.broadcast_to(null_kv[1], (b, 1, DIM_HEAD))
        k = jnp.concatenate([nk, k], axis=1)
        v = jnp.concatenate([nv, v], axis=1)
        q = l2norm(q) * q_scale
        k = l2norm(k) * k_scale
        sim = jnp.einsum('bhid,bjd->bhij', q, k) * SCALE
        bias = rel_pos_bias(n, w0, b0, g0, w1, b1, g1, w2, b2, q.dtype)
        null_bias = jnp.broadcast_to(null_attn_bias[:, None, None], (HEADS, n, 1))
        attn_bias = jnp.concatenate([null_bias, bias], axis=-1)
        sim = sim + attn_bias
        neg = -jnp.finfo(sim.dtype).max
        causal = jnp.triu(jnp.ones((n, n + 1), dtype=bool), k=2)
        sim = jnp.where(causal, neg, sim)
        m = jnp.pad(mask, ((0, 0), (1, 0)), constant_values=True)[:, None, None, :]
        sim = jnp.where(m, sim, neg)
        attn = jax.nn.softmax(sim, axis=-1)
        out = jnp.einsum('bhij,bjd->bhid', attn, v)
        out = out.transpose(0, 2, 1, 3).reshape(b, n, HEADS * DIM_HEAD)
        return ln(out @ Wout, g_out)
    x = x + _L0_cond_ref(x, mask_BxS_bf1, L0_cond_g_norm, L0_cond_Wq, L0_cond_Wkv, L0_cond_q_scale, L0_cond_k_scale, cond_64, L0_cond_null_attn_bias, L0_cond_w0, L0_cond_b0, L0_cond_g0, L0_cond_w1, L0_cond_b1, L0_cond_g1, L0_cond_w2, L0_cond_b2, L0_cond_Wout, L0_cond_g_out)
    return x

_drawn_inputs = setup_inputs


def setup_inputs(seed=0):
    import zlib

    import numpy as np

    out = dict(_drawn_inputs(seed))
    spreads = {'L0_cond_g_norm': (1.0, 0.2),
     'L0_cond_q_scale': (1.0, 0.2),
     'L0_cond_k_scale': (1.0, 0.2),
     'L0_cond_b0': (0.0, 0.286),
     'L0_cond_g0': (1.0, 0.6),
     'L0_cond_b1': (0.0, 0.412),
     'L0_cond_g1': (1.0, 0.6),
     'L0_cond_b2': (0.0, 0.8),
     'L0_cond_g_out': (1.0, 0.2)}
    factors = {}
    for name, (base, spread) in spreads.items():
        noise = np.random.default_rng([zlib.crc32(name.encode()), seed]).standard_normal(out[name].shape)
        drawn = base * np.exp(spread * noise) if base else spread * noise
        out[name] = jnp.asarray(drawn.astype(out[name].dtype))
    for name, factor in factors.items():
        out[name] = (out[name] * factor).astype(out[name].dtype)
    return out
```

```python
import numpy as np
import concourse.bass as bass
from concourse import mybir
from contextlib import ExitStack

B, N, D = 8, 512, 512
H, DH = 16, 64
P = 128
Q = 32
T = N // P
KC = D // P
PAIRS = H // 2
CH = 2
HC = H // CH
SCALE = 8.0
EPS = 1e-5
MASKED = 1e30
PADK = 32768.0
RW = N + P
HEADSLOTS = 4
GROUPS = 5
PSLOTS = 4
S_AT = [P * t * (t + 1) // 2 for t in range(T)]
S_N = [P * (t + 1) for t in range(T)]
S_ALL = sum(S_N)
GROUP = [[(0, 0, 0)], [(0, 1, 0), (0, 3, 384)], [(1, 0, 0)], [(1, 1, 0), (1, 3, 384)], [(0, 2, 0), (1, 2, 256)]]
PV_SETS = [[(0, ((0, 0), (2, 0)))], [(1, ((1, 0), (3, 0))), (3, ((1, 384), (3, 384)))], [(2, ((4, 0), (4, 256)))]]
PV_NEEDS = [2, 3, 4]
PV_FREES = {0: 0, 2: 0, 1: 1, 3: 1, 4: 2}
ORDER = [("qt", 0), ("qk", 0), ("qk", 1), ("fill", 0), ("qk", 2), ("pt", 0), ("qk", 3), ("pt", 1),
         ("qk", 4), ("fill", 1), ("qk", 5), ("pt", 2), ("null", 0), ("qk", 6), ("pt", 3), ("qk", 7),
         ("fill", 2), ("pt", 4), ("pv", 0), ("null", 1), ("pv", 1), ("pv", 2)]
TILE_OF = [(0, 3), (0, 2), (0, 1), (0, 0), (1, 3), (1, 2), (1, 1), (1, 0)]
FILL = {
    1: [[("q1", 0)], [("q1", 1)], []],
    2: [[("q1", 2)], [("q1", 3)], []],
    3: [[("xt", 0), ("xt", 1)], [("xt", 2), ("xt", 3)], [("kv", 0)]],
    4: [[("nul", 0)], [("kvn", 0)], [("nn", 0)]],
    5: [[("q0", 0)], [("q0", 1)], []],
    6: [[("q0", 2)], [("q0", 3)], []],
    7: [[], [("pnt", 0)], []],
    0: [[("c", 0)], [("c", 1)], [("c", 2), ("c", 3)]],
}


def at(b, per, n):
    return b * per + n


def wait(eng, sem, value):
    if isinstance(value, int) and value <= 0:
        return
    eng.wait_ge(sem, value)


G_USE = {"xt": 0, "kv": 4, "nul": 5, "kvn": 6, "nn": 7, "q0": 8, "kt": 12, "q1": 13, "pnt": 30, "c": 31}
G_PER = 22


def g_use(b, name, i):
    k = G_USE[name] + i
    if name in ("xt", "kv", "nul", "kvn", "nn", "q0", "kt"):
        if not (isinstance(b, int) and b == 0):
            k -= 5
    if name in ("pnt", "c") and isinstance(b, int) and b == B - 1:
        k -= 13
    return k % 2, b * (G_PER // 2) + k // 2


def build(nc, x, cond, mask, g_norm, Wq, Wkv, q_scale, k_scale, null_bias,
          w0, b0, g0, w1, b1, g1, w2, b2, Wout, g_out, out):
    F32, F32R, F16, U8 = mybir.dt.float32, mybir.dt.float32r, mybir.dt.float16, mybir.dt.uint8
    ALU, ACT, AX = mybir.AluOpType, mybir.ActivationFunctionType, mybir.AxisListType

    table = nc.dram_tensor("bias_table", (H, P * RW), F32).ap()

    ctx = ExitStack()
    with ctx:
        def sb(name, shape, dt=F32):
            return ctx.enter_context(nc.sbuf_tensor(name, shape, dt))

        def pb(name, shape, dt=F32):
            return ctx.enter_context(nc.psum_tensor(name, shape, dt))

        def sem(name):
            return ctx.enter_context(nc.semaphore(name))

        wq_hi = sb("wq_hi", [P, KC, H * DH], F32R)
        wq_lo = sb("wq_lo", [P, KC, H * DH], F32R)
        wkv_hi = sb("wkv_hi", [P, KC, H + 2 * DH], F32R)
        wkv_lo = sb("wkv_lo", [P, KC, H + 2 * DH], F32R)
        wo_hi = sb("wo_hi", [P, PAIRS, D], F32R)
        wo_lo = sb("wo_lo", [P, PAIRS, D], F32R)
        nvw = sb("nvw", [3 * Q, D], F32R)
        ident = sb("ident", [P, P])
        ident16 = sb("ident16", [P, P], F16)
        half = sb("half", [P, H])
        eps = sb("eps", [P, T])
        g_col = sb("g_col", [P, KC])
        gout_row = sb("gout_row", [P, D])
        nb_row = sb("nb_row", [P, H])
        s_row = sb("s_row", [P, DH])
        nk_row = sb("nk_row", [P, DH])
        ks_row = sb("ks_row", [P, DH])
        xs = sb("xs", [P, 2, D])
        xt_hi = sb("xt_hi", [P, KC, N], F32R)
        xt_lo = sb("xt_lo", [P, KC, N], F32R)
        bn6 = sb("bn6", [P, T, 6])
        mv = sb("mv", [P, T, 2])
        ve = sb("ve", [P, T])
        rstd = sb("rstd", [P, T])
        kvt = xs[:, 0, :]
        nt = sb("nt", [H, RW])
        kss = sb("kss", [P, T])
        kssg = sb("kssg", [P, T])
        rk = sb("rk", [P, T])
        knat = sb("knat", [P, T, 3 * DH], F16)
        vst = sb("vst", [P, T, DH])
        v = sb("v", [P, T, DH])
        ka = sb("ka", [P, N], F16)
        kb = sb("kb", [P, N], F16)
        mask_u8 = sb("mask_u8", [P, N], U8)
        nsr = sb("nsr", [P, T, H])
        qsq = sb("qsq", [P, HC, DH])
        qss = sb("qss", [P, HC])
        qssg = sb("qssg", [P, HC])
        rq = sb("rq", [P, HC])
        nsq = sb("nsq", [P, HC])
        qf = sb("qf", [P, HC, DH])
        ksq, kh = qsq[:, 0:T, :], qf[:, 0:T, :]
        qn = [sb(f"qn{c}", [P, T, HC, 2 * DH], F16) for c in range(CH)]
        nsn = sb("nsn", [P, T, H])
        qa = [sb(f"qa{i}", [P, 2, N], F16) for i in range(2)]
        qb = [sb(f"qb{i}", [DH + 1, 2, N], F16) for i in range(2)]
        tb = [sb(f"tb{i}", [P, 2, N]) for i in range(2)]
        pr = sb("pr", [P, HEADSLOTS, S_ALL])
        mn = sb("mn", [P, HEADSLOTS, T])
        rs = sb("rs", [P, HEADSLOTS, T])
        dn = sb("dn", [P, HEADSLOTS, T])
        pn = sb("pn", [P, HEADSLOTS, T])
        den = sb("den", [P, HEADSLOTS, T])
        rr = sb("rr", [P, HEADSLOTS, T])
        pnat = sb("pnat", [P, T, H])
        pts = sb("pts", [P, PSLOTS, N])
        ot_hi = sb("ot_hi", [P, PAIRS, N], F32R)
        ot_lo = sb("ot_lo", [P, PAIRS, N], F32R)
        pnt = sb("pnt", [3 * Q, N], F32R)
        cbn6 = sb("cbn6", [P, 6])
        cmv = sb("cmv", [P, 2])
        cve = sb("cve", [P, 1])
        crs = sb("crs", [P, 1])
        res = [sb(f"res{i}", [P, D]) for i in range(2)]

        ps_s = [pb(f"ps_s{i}", [P, N]) for i in range(2)]
        ps_pt = [pb(f"ps_pt{i}", [P, N]) for i in range(2)]
        ps_o = pb("ps_o", [P, N])
        ps_g = [pb(f"ps_g{i}", [P, N]) for i in range(2)]
        ps_qt = pb("ps_qt", [P, 2, N], F16)

        z = pr[:, :, :].rearrange("p a b -> p (a b)")[:, 0:T * D].rearrange("p (t d) -> p t d", t=T)
        ez = pr[:, :, :].rearrange("p a b -> p (a b)")[:, T * D:2 * T * D].rearrange("p (t d) -> p t d", t=T)
        row_w0, row_b0, row_g0, row_b1 = (tb[i // 2][:, i % 2, :] for i in range(4))
        row_g1 = res[0][:, :]
        w1_sb = qn[0][:, :, :, :].rearrange("p a b c -> p (a b c)").bitcast(F32).rearrange("p (k n) -> p k n", k=KC)
        ht = qn[1][:, :, :, :].rearrange("p a b c -> p (a b c)").bitcast(F32).rearrange("p (k n) -> p k n", k=KC)
        stage = [pts[:, 2 * i:2 * i + 2, :].rearrange("p a b -> p (a b)") for i in range(2)]
        prod = xs[:, :, :].rearrange("p a b -> p (a b)")
        w2_sb = vst[:, 0, :].rearrange("p (k h) -> p k h", k=KC)
        wn = vst[:, 1, :].rearrange("p (k h) -> p k h", k=KC)
        nv_blk = vst[:, 2:4, :].rearrange("p a (q h) -> p (a q) h", h=H)
        b2_col = sb("b2_col", [H, 1])
        nv_col = sb("nv_col", [P, 1])
        tab = nt
        dist = sb("dist", [P, T])
        nk_sq = qsq[:, 0, :]
        nk_ss = sb("nk_ss", [P, 3])

        consts = sem("consts"); id_zero = sem("id_zero"); id_made = sem("id_made")
        rows_in = sem("rows_in"); w1_in = sem("w1_in")
        stage_in = [sem("stage_in0"), sem("stage_in1")]
        hi_made = sem("hi_made"); stage_read = sem("stage_read"); nvw_acc = sem("nvw_acc")
        vec = sem("vec"); nk_pow = sem("nk_pow"); wn_made = sem("wn_made")
        nvw_hi_made = sem("nvw_hi_made"); zeros = sem("zeros"); weights = sem("weights")
        z_sum = sem("z_sum"); z_stats = sem("z_stats"); z_mv = sem("z_mv"); z_ve = sem("z_ve"); z_rstd = sem("z_rstd")
        z_norm = sem("z_norm"); z_gain = sem("z_gain"); z_exp = sem("z_exp"); z_step = sem("z_step"); z_act = sem("z_act")
        h_turned = sem("h_turned"); h_drained = sem("h_drained"); h_mm = sem("h_mm"); tab_ps = sem("tab_ps"); tab_made = sem("tab_made")
        tab_out = sem("tab_out")
        passed = sem("passed")
        x_in = [sem("x_in0"), sem("x_in1")]; stats = sem("stats"); mv_ready = sem("mv_ready"); ve_made = sem("ve_made"); rstd_ready = sem("rstd_ready")
        xn_ready = sem("xn_ready"); xt_ps = sem("xt_ps"); xt_hi_made = sem("xt_hi_made")
        kv_ps = sem("kv_ps"); nul_ps = sem("nul_ps"); kvn_ps = sem("kvn_ps"); nn_ps = sem("nn_ps")
        ksq_made = sem("ksq_made"); kss_made = sem("kss_made"); kssg_made = sem("kssg_made"); rk_ready = sem("rk_ready")
        khi_made = sem("khi_made"); kn_ready = sem("kn_ready"); kt_ps = sem("kt_ps"); mask_in = sem("mask_in")
        kv_ready = sem("kv_ready"); v_ready = sem("v_ready"); vst_made = sem("vst_made")
        q_ps = sem("q_ps"); qsq_made = sem("qsq_made"); qss_made = sem("qss_made"); qssg_made = sem("qssg_made"); rq_ready = sem("rq_ready")
        nsq_made = sem("nsq_made"); nsn_ready = sem("nsn_ready"); qhi_made = sem("qhi_made"); qn_ready = sem("qn_ready")
        g_drained = [sem("g_drained0"), sem("g_drained1")]
        qt_ps = sem("qt_ps"); qa_ready = sem("qa_ready"); qb_ready = sem("qb_ready")
        tb_in = [sem("tb_in0"), sem("tb_in1")]
        qk_ps = sem("qk_ps"); biased = sem("biased"); exp_done = sem("exp_done")
        dn_ready = sem("dn_ready"); pn_ready = sem("pn_ready"); den_ready = sem("den_ready"); rr_ready = sem("rr_ready")
        normed = sem("normed"); pnat_ready = sem("pnat_ready"); pt_ps = sem("pt_ps"); pt_drained = [sem("pt_drained0"), sem("pt_drained1")]
        pv_done = sem("pv_done"); oh_made = sem("oh_made"); o_drained = sem("o_drained")
        pnt_ps = sem("pnt_ps"); pnh_made = sem("pnh_made"); c_ps = sem("c_ps"); cstats = sem("cstats")
        cmv_ready = sem("cmv_ready"); cve_made = sem("cve_made"); crs_ready = sem("crs_ready"); og_made = sem("og_made")
        res_in = [sem("res_in0"), sem("res_in1")]; out_sent = [sem("out_sent0"), sem("out_sent1")]

        def slot(p, h):
            return (2 * p + h) % HEADSLOTS

        def slot_free(n):
            p, g = divmod(n - PSLOTS, GROUPS)
            return 3 * p + PV_FREES[g] + 1

        def wait_apart(sem, value):
            nc.vector.wait_ge(sem, value)
            nc.vector.sem_inc(passed, 1)

        def drained(eng, b, name, i):
            bank, before = g_use(b, name, i)
            eng.wait_ge(g_drained[bank], before + 1)

        def claim(eng, b, name, i):
            bank, before = g_use(b, name, i)
            wait(eng, g_drained[bank], before)
            return ps_g[bank]

        def bank_of(b, name, i):
            return ps_g[g_use(b, name, i)[0]], g_drained[g_use(b, name, i)[0]]

        def iterations(eng, run):
            def batch(b):
                for p in range(1, PAIRS):
                    run(b, p)

            run(0, -1)
            run(0, 0)
            batch(0)
            run(1, 0)
            with eng.Fori(1, B - 1) as b:
                batch(b)
                run(b + 1, 0)
            batch(B - 1)

        def following(b, p):
            if p == PAIRS - 1:
                return (None, None) if last(b) else (b + 1, 0)
            return b, p + 1

        def fillers(b, p, k):
            if p < 0 or (p == 0 and first(b)):
                return
            for name, i in FILL[p][k]:
                if name == "c":
                    yield name, i, b - 1
                elif name in ("q1", "pnt"):
                    yield name, i, b
                elif not last(b):
                    yield name, i, b + 1

        def first_projections():
            for name, n in (("xt", T), ("kv", 1), ("nul", 1), ("kvn", 1), ("nn", 1), ("q0", T)):
                for i in range(n):
                    yield name, i

        def first(b):
            return isinstance(b, int) and b == 0

        def last(b):
            return isinstance(b, int) and b == B - 1

        block = ctx.enter_context(nc.Block())

        @block.sync
        def _(sp):
            def load_x(b, tiles):
                for t in tiles:
                    wait(sp, weights, 0 if first(b) else 1)
                    wait(sp, xt_ps, at(b, T, t - 1))
                    if t == 0:
                        wait(sp, kvn_ps, at(b, 1, 0))
                    sp.dma_start(xs[:, t % 2, :], x[bass.ds(b, 1), t * P:(t + 1) * P, :].rearrange("a p d -> (a p) d")
                                 ).then_inc(x_in[t % 2], 16)

            for dst, src in ((row_w0, w0[0, :]), (row_b0, b0), (row_g0, g0), (row_b1, b1), (row_g1, g1),
                             (nk_row[:], cond[0, :]), (s_row[:], q_scale), (ks_row[:], k_scale),
                             (nb_row[:], null_bias), (gout_row[:], g_out)):
                sp.dma_start(dst, src.partition_broadcast(P)).then_inc(rows_in, 16)
            sp.dma_start(w2_sb, w2.rearrange("(k p) h -> p k h", p=P)).then_inc(rows_in, 16)
            sp.dma_start(b2_col[:], b2.unsqueeze(1)).then_inc(rows_in, 16)
            sp.dma_start(g_col[:], g_norm.rearrange("(k p) -> p k", p=P),
                         allow_slow_non_contiguous=True).then_inc(rows_in, 16)
            for h in range(2):
                sp.dma_start(nv_col[h * DH:(h + 1) * DH, :], cond[1, :].unsqueeze(1)).then_inc(rows_in, 16)
            sp.dma_start(w1_sb, w1.rearrange("(k p) n -> p k n", p=P)).then_inc(w1_in, 16)
            for k in range(2 * KC + 1):
                wait(sp, stage_read, k - 1)
                wait(sp, nvw_acc, k - 2 - KC)
                if k < KC:
                    dst, src = stage[k % 2], Wq[k * P:(k + 1) * P, :]
                elif k == KC:
                    dst = stage[0][:, 0:KC * 2 * DH].rearrange("p (k n) -> p k n", k=KC)
                    src = Wkv.rearrange("(k p) n -> p k n", p=P)
                else:
                    j = k - KC - 1
                    dst = stage[k % 2].rearrange("p (a n) -> p a n", a=2)
                    src = Wout[2 * j * P:2 * (j + 1) * P, :].rearrange("(a p) n -> p a n", p=P)
                sp.dma_start(dst, src).then_inc(stage_in[k % 2], 16)
            sp.wait_ge(tab_made, 2)
            for h in range(H):
                sp.dma_start(table[h:h + 1, :].rearrange("a (p u) -> a p u", p=P),
                             tab[h:h + 1, :].unsqueeze(1).broadcast_to([1, P, RW])).then_inc(tab_out, 16)
            sp.wait_ge(tab_out, 16 * H)
            sp.wait_ge(wn_made, KC)
            load_x(0, range(T))
            sp.dma_start(mask_u8[DH:DH + 1, :], mask[0:1, :]).then_inc(mask_in, 16)

            def load_bias(b, p):
                wait(sp, weights, 0 if first(b) else 1)
                wait(sp, biased, at(b, 64, 8 * (p - 1)))
                src = bass.AP(table.tensor, 2 * p * P * RW + P - 1, [[RW - 1, P], [P * RW, 2], [1, N]])
                sp.dma_start(tb[p % 2][:], src).then_inc(tb_in[p % 2], 16)

            def store(b):
                for t in range(2):
                    load_rows(b, t)
                for t in range(T):
                    sp.wait_ge(weights, 1)
                    drained(sp, b, "c", t)
                    sp.dma_start(out[bass.ds(b, 1), t * P:(t + 1) * P, :].rearrange("a p d -> (a p) d"), res[t % 2][:]
                                 ).then_inc(out_sent[t % 2], 16)
                    if t + 2 < T:
                        load_rows(b, t + 2)

            def load_rows(b, t):
                    sp.wait_ge(weights, 1)
                    wait(sp, out_sent[t % 2], at(b, 16 * (T // 2), 16 * (t // 2)))
                    sp.dma_start(res[t % 2][:], x[bass.ds(b, 1), t * P:(t + 1) * P, :].rearrange("a p d -> (a p) d")
                                 ).then_inc(res_in[t % 2], 16)

            def run(b, p):
                if p == -1:
                    load_bias(b, 0)
                    load_bias(b, 1)
                    return
                fb, fp = following(*following(b, p)) if not (last(b) and p == PAIRS - 1) else (None, None)
                if fb is not None:
                    load_bias(fb, fp)
                if p == 0 and not first(b):
                    store(b - 1)
                if p == 1 and not last(b):
                    load_x(b + 1, (0, 1))
                    sp.wait_ge(weights, 1)
                    sp.wait_ge(kv_ready, at(b, 1, 1))
                    sp.dma_start(mask_u8[DH:DH + 1, :], mask[bass.ds(b + 1, 1), :]).then_inc(mask_in, 16)
                if p == 3 and not last(b):
                    load_x(b + 1, (2, 3))

            iterations(sp, run)
            store(B - 1)
            for i in range(2):
                sp.wait_ge(out_sent[i], 16 * (T // 2) * B)

        @block.tensor
        def _(pe):
            pe.wait_ge(consts, 4)
            pe.wait_ge(id_made, 2)
            banks = [ps_s[0], ps_s[1], ps_pt[0], ps_pt[1]]
            for layer in range(2):
                pe.wait_ge(z_act, layer + 1)
                for m in range(T):
                    for k in range(KC):
                        mm = pe.transpose(banks[m][:, k * P:(k + 1) * P], z[:, m, k * P:(k + 1) * P], ident[:])
                    mm.then_inc(h_turned, 1)
                pe.wait_ge(h_drained, T * (layer + 1))
                if layer == 0:
                    pe.wait_ge(w1_in, 16)
                    for m in range(T):
                        for k in range(KC):
                            mm = pe.matmul(banks[m][:], ht[:, k, m * P:(m + 1) * P], w1_sb[:, k, :],
                                           start=k == 0, stop=k == KC - 1)
                        mm.then_inc(h_mm, 1)
                else:
                    pe.wait_ge(rows_in, ROWS_IN)
                    for k in range(KC):
                        mm = pe.matmul(ps_o[0:H, :], w2_sb[:, k, :], ht[:, k, :], start=k == 0, stop=k == KC - 1)
                    mm.then_inc(tab_ps, 1)
            pe.wait_ge(vec, 7)
            for j in range(PAIRS // 2):
                k = KC + 1 + j
                pe.wait_ge(stage_in[k % 2], 16 * (k // 2 + 1))
                for a in range(2):
                    q = 2 * j + a
                    mm = pe.matmul(ps_g[0][0:H, :], nv_blk[:, q, :], stage[k % 2][:, a * D:(a + 1) * D],
                                   start=q == 0, stop=q == PAIRS - 1)
                mm.then_inc(nvw_acc, 1)
            pe.wait_ge(weights, 1)

            def turn_x(b, t):
                bank = claim(pe, b, "xt", t)
                pe.wait_ge(xn_ready, at(b, T, t + 1))
                for k in range(KC):
                    mm = pe.transpose(bank[:, k * P:(k + 1) * P], xs[:, t % 2, k * P:(k + 1) * P], ident[:])
                mm.then_inc(xt_ps, 1)

            def products(bank, pairs):
                for i, (lhs, rhs) in enumerate(pairs):
                    mm = pe.matmul(bank, lhs, rhs, start=i == 0, stop=i == len(pairs) - 1)
                return mm

            def keys_values(b, name, done, col):
                bank = claim(pe, b, name, 0)
                for t in range(T):
                    drained(pe, b, "xt", t)
                cols = slice(col, col + P)
                products(bank[:], [(w[:, k, cols], xt[:, k, :]) for k in range(KC)
                                   for w, xt in ((wkv_hi, xt_hi), (wkv_lo, xt_hi), (wkv_hi, xt_lo))]).then_inc(done, 1)

            def turn_kv(b):
                bank = claim(pe, b, "kvn", 0)
                drained(pe, b, "kv", 0)
                for t in range(T):
                    mm = pe.transpose(bank[:, t * P:(t + 1) * P], kvt[:, t * P:(t + 1) * P], ident[:])
                mm.then_inc(kvn_ps, 1)

            def turn_null(b):
                bank = claim(pe, b, "nn", 0)
                drained(pe, b, "nul", 0)
                pe.transpose(bank[:, P:2 * P], ident[:], ident[:])
                for t in range(T):
                    mm = pe.transpose(bank[:, t * H:(t + 1) * H], nt[:, t * P:(t + 1) * P], ident[0:H, 0:H])
                mm.then_inc(nn_ps, 1)

            def turn_k(b):
                bank = claim(pe, b, "kt", 0)[:, :].bitcast(F16)
                pe.wait_ge(kn_ready, at(b, 1, 1))
                for t in range(T):
                    pe.transpose(bank[:, t * P:(t + 1) * P], knat[:, t, 0:2 * DH], ident16[:])
                for t in range(T):
                    mm = pe.transpose(bank[0:DH, N + t * P:N + (t + 1) * P], knat[:, t, 2 * DH:3 * DH], ident16[:])
                mm.then_inc(kt_ps, 1)

            def project_q(b, c, t):
                bank = claim(pe, b, f"q{c}", t)
                if c == 0 and t == 0:
                    for i in range(T):
                        drained(pe, b, "xt", i)
                rows, cols = slice(t * P, (t + 1) * P), slice(c * HC * DH, (c + 1) * HC * DH)
                products(bank[:], [(xt[:, k, rows], w[:, k, cols]) for k in range(KC)
                                   for xt, w in ((xt_hi, wq_hi), (xt_hi, wq_lo), (xt_lo, wq_hi))]).then_inc(q_ps, 1)

            def turn_q(b, p):
                c, h = p // (HC // 2), 2 * (p % (HC // 2))
                pe.wait_ge(qn_ready, at(b, 2 * T, T * c + T))
                wait(pe, qb_ready, at(b, PAIRS, p))
                for i in range(2):
                    for t in range(T):
                        mm = pe.transpose(ps_qt[:, i, t * P:(t + 1) * P], qn[c][:, t, h + i, :], ident16[:])
                mm.then_inc(qt_ps, 1)

            def scores(b, p, i):
                h, t = TILE_OF[i]
                if i == 0:
                    pe.wait_ge(qb_ready, at(b, PAIRS, p + 1))
                    pe.wait_ge(kv_ready, at(b, 1, 1))
                wait(pe, biased, at(b, 64, 8 * p + i - 1))
                o = ps_s[i % 2][:, 0:S_N[t]]
                rows = slice(t * P, (t + 1) * P)
                pe.matmul(o, qa[p % 2][:, h, rows], ka[:, 0:S_N[t]], start=True, stop=False)
                pe.matmul(o, qb[p % 2][:, h, rows], kb[0:DH + 1, 0:S_N[t]], start=False, stop=True).then_inc(qk_ps, 1)

            def turn_probs(b, p, g):
                n = GROUPS * p + g
                pe.wait_ge(normed, at(b, H, 2 * p + 1 + max(h for h, _, _ in GROUP[g])))
                wait(pe, pt_drained[n % 2], at(b, 20, n // 2))
                for h, kb_, col in GROUP[g]:
                    for t in range(kb_, T):
                        at_ = S_AT[t] + kb_ * P
                        mm = pe.transpose(ps_pt[n % 2][:, col + (t - kb_) * P:col + (t - kb_ + 1) * P],
                                          pr[:, slot(p, h), at_:at_ + P], ident[:])
                mm.then_inc(pt_ps, 1)

            def weigh_values(b, p, s):
                n = GROUPS * p + PV_NEEDS[s]
                for m in range(max(0, n - 1), n + 1):
                    pe.wait_ge(pt_drained[m % 2], at(b, 20, m // 2 + 1))
                if s == 0:
                    wait(pe, o_drained, at(b, PAIRS, p))
                    if p == 0:
                        pe.wait_ge(v_ready, at(b, 1, 1))
                for kb_, places in PV_SETS[s]:
                    for h, (g, col) in enumerate(places):
                        w = (T - kb_) * P
                        mm = pe.matmul(ps_o[h * DH:(h + 1) * DH, kb_ * P:N], v[:, kb_, :], pts[:, (GROUPS * p + g) % PSLOTS, col:col + w],
                                       start=kb_ == 0, stop=kb_ == 2)
                mm.then_inc(pv_done, 1)

            def turn_null_probs(b):
                bank = claim(pe, b, "pnt", 0)
                pe.wait_ge(pnat_ready, at(b, H, H))
                for t in range(T):
                    mm = pe.transpose(bank[0:H, t * P:(t + 1) * P], pnat[:, t, :], ident[:])
                mm.then_inc(pnt_ps, 1)

            def project_out(b, t):
                bank = claim(pe, b, "c", t)
                if t == 0:
                    pe.wait_ge(o_drained, at(b, PAIRS, PAIRS))
                    drained(pe, b, "pnt", 0)
                rows = slice(t * P, (t + 1) * P)
                parts = [(o[:, q, rows], w[:, q, :]) for q in range(PAIRS)
                         for o, w in ((ot_hi, wo_hi), (ot_hi, wo_lo), (ot_lo, wo_hi))]
                parts += [(pnt[:, rows], nvw[:])]
                products(bank[:], parts).then_inc(c_ps, 1)

            def fill(name, i, b):
                if name == "xt":
                    turn_x(b, i)
                elif name == "kv":
                    keys_values(b, "kv", kv_ps, H)
                elif name == "nul":
                    keys_values(b, "nul", nul_ps, 0)
                elif name == "kvn":
                    turn_kv(b)
                elif name == "nn":
                    turn_null(b)
                elif name in ("q0", "q1"):
                    project_q(b, int(name[1]), i)
                elif name == "pnt":
                    turn_null_probs(b)
                else:
                    project_out(b, i)

            def run(b, p):
                fb, fp = following(b, p)
                for what, i in ORDER:
                    if what == "qt" and fb is not None:
                        if fp == 0:
                            turn_k(fb)
                        turn_q(fb, fp)
                    elif what == "qk" and fb is not None:
                        scores(fb, fp, i)
                    elif what == "fill":
                        for f in fillers(b, p, i):
                            fill(*f)
                    elif what == "pt" and p >= 0:
                        turn_probs(b, p, i)
                    elif what == "pv" and p >= 0:
                        weigh_values(b, p, i)

            for name, i in first_projections():
                fill(name, i, 0)
            iterations(pe, run)
            for t in range(T):
                project_out(B - 1, t)

        @block.scalar
        def _(act):
            def hi_weights(k):
                act.wait_ge(stage_in[k % 2], 16 * (k // 2 + 1))
                if k < KC:
                    act.activation(wq_hi[:, k, :], stage[k % 2], ACT.Copy, scale=g_col[:, k:k + 1]).then_inc(hi_made, 1)
                elif k == KC:
                    act.wait_ge(wn_made, KC)
                    for j in range(KC):
                        act.activation(wkv_hi[:, j, H:], stage[0][:, j * P:(j + 1) * P], ACT.Copy, scale=g_col[:, j:j + 1])
                        a = act.activation(wkv_hi[:, j, 0:H], wn[:, j, :], ACT.Copy, scale=g_col[:, j:j + 1])
                    a.then_inc(hi_made, 1)
                else:
                    j = k - KC - 1
                    act.activation(wo_hi[:, 2 * j:2 * j + 2, :].rearrange("p a n -> p (a n)"), stage[k % 2], ACT.Copy
                                   ).then_inc(hi_made, 1)

            act.wait_ge(rows_in, ROWS_IN)
            for layer in range(2):
                act.wait_ge(z_gain, layer + 1)
                act.activation(ez, z, ACT.Exp, scale=-1.0).then_inc(z_exp, 1)
                for m in range(T):
                    act.wait_ge(h_turned, T * layer + m + 1)
                    act.activation(ht[:, :, m * P:(m + 1) * P],
                                   [ps_s[0], ps_s[1], ps_pt[0], ps_pt[1]][m][:, :].rearrange("p (k n) -> p k n", k=KC),
                                   ACT.Copy).then_inc(h_drained, 1)
                if layer == 0:
                    for k in range(KC):
                        hi_weights(k)
            for k in range(KC, 2 * KC + 1):
                hi_weights(k)
            act.wait_ge(nvw_acc, PAIRS // 2)
            act.wait_ge(zeros, 2)
            act.activation(nvw[0:H, :], ps_g[0][0:H, :], ACT.Copy)
            act.activation(nvw[2 * Q:2 * Q + H, :], ps_g[0][0:H, :], ACT.Copy).then_inc(nvw_hi_made, 1)

            def fill(name, i, b):
                if name == "xt":
                    bank, _ = bank_of(b, name, i)
                    act.wait_ge(xt_ps, at(b, T, i + 1))
                    act.activation(xt_hi[:, :, i * P:(i + 1) * P], bank[:, :].rearrange("p (k n) -> p k n", k=KC),
                                   ACT.Copy).then_inc(xt_hi_made, 1)
                elif name == "kv":
                    bank, done = bank_of(b, name, i)
                    act.wait_ge(kv_ps, at(b, 1, 1))
                    act.activation(kvt, bank[:], ACT.Copy).then_inc(done, 1)
                elif name == "nul":
                    bank, done = bank_of(b, name, i)
                    act.wait_ge(nul_ps, at(b, 1, 1))
                    act.wait_ge(tab_out, 16 * H)
                    act.activation(nt[:, 0:N], bank[0:H, :], ACT.Copy).then_inc(done, 1)
                elif name == "kvn":
                    bank, _ = bank_of(b, name, i)
                    act.wait_ge(kvn_ps, at(b, 1, 1))
                    wait(act, qss_made, at(b, 2 * T, 0))
                    act.activation(ksq, bank[:, :].rearrange("p (t n) -> p t n", t=T)[:, :, 0:DH],
                                   ACT.Square).then_inc(ksq_made, 1)
                elif name in ("q0", "q1"):
                    n = at(b, 2 * T, T * int(name[1]) + i)
                    bank, _ = bank_of(b, name, i)
                    wait(act, qss_made, n)
                    act.wait_ge(kss_made, at(b, 1, 1))
                    act.wait_ge(q_ps, n + 1)
                    act.activation(qsq[:], bank[:, :].rearrange("p (h d) -> p h d", h=HC), ACT.Square).then_inc(qsq_made, 1)
                elif name == "pnt":
                    bank, _ = bank_of(b, name, i)
                    act.wait_ge(pnt_ps, at(b, 1, 1))
                    act.activation(pnt[0:H, :], bank[0:H, :], ACT.Copy)
                    act.activation(pnt[Q:Q + H, :], bank[0:H, :], ACT.Copy).then_inc(pnh_made, 1)

            def run(b, p):
                fb, fp = following(b, p)
                for what, i in ORDER:
                    if what == "qt" and fb is not None:
                        act.wait_ge(qa_ready, at(fb, PAIRS, fp + 1))
                        act.activation(qb[fp % 2][0:DH], ps_qt[0:DH], ACT.Copy).then_inc(qb_ready, 1)
                    elif what == "qk" and fb is not None:
                        h, t = TILE_OF[i]
                        s = slot(fp, h)
                        act.wait_ge(biased, at(fb, 64, 8 * fp + i + 1))
                        if i % T == 0:
                            wait(act, den_ready, at(fb, H, 2 * fp + h - HEADSLOTS + 1))
                        e = pr[:, s, S_AT[t]:S_AT[t] + S_N[t]]
                        act.activation(e, e, ACT.Exp, bias=mn[:, s, t:t + 1], scale=-1.0,
                                       accum_out=rs[:, s, t:t + 1]).then_inc(exp_done, 1)
                    elif what == "null" and fb is not None:
                        s = slot(fp, i)
                        act.wait_ge(dn_ready, at(fb, H, 2 * fp + i + 1))
                        act.activation(pn[:, s, :], dn[:, s, :], ACT.Exp, scale=-1.0).then_inc(pn_ready, 1)
                    elif what == "fill":
                        for f in fillers(b, p, i):
                            fill(*f)
                    elif what == "pt" and p >= 0 and (GROUPS * p + i) % 2 == 0:
                        drain_group(act, b, p, i)
                    elif what == "pv" and i == 2 and p >= 0:
                        act.wait_ge(pv_done, at(b, 3 * PAIRS, 3 * p + 3))
                        if p == 0:
                            wait(act, c_ps, at(b, T, 0))
                        act.activation(ot_hi[:, p, :], ps_o[:], ACT.Copy).then_inc(oh_made, 1)

            def drain_group(act, b, p, g):
                n = GROUPS * p + g
                act.wait_ge(pt_ps, at(b, GROUPS * PAIRS, n + 1))
                wait(act, pv_done, at(b, 3 * PAIRS, slot_free(n)))
                act.activation(pts[:, n % PSLOTS, :], ps_pt[0][:], ACT.Copy).then_inc(pt_drained[0], 1)

            for name, i in first_projections():
                fill(name, i, 0)
            iterations(act, run)

        @block.gpsimd
        def _(pool):
            pool.memset(ident[:], 0.0).then_inc(id_zero, 1)
            pool.memset(half[:], -0.5).then_inc(consts, 1)
            pool.memset(eps[:], EPS).then_inc(consts, 1)
            pool.memset(nv_blk, 0.0).then_inc(consts, 1)
            pool.iota(dist[:], pattern=[[-P, T]], base=N - 1, channel_multiplier=-1,
                      allow_small_or_imprecise_dtypes=True).then_inc(consts, 1)
            pool.wait_ge(id_zero, 1)
            pool.affine_select(out=ident[:], in_=ident[:], compare_op=ALU.not_equal, fill=1.0, base=0,
                               pattern=[[-1, P]], channel_multiplier=1).then_inc(id_made, 1)
            pool.wait_ge(consts, 4)

            def root(dst, src, width, ready):
                pool.tensor_tensor(dst, src, half[:, 0:width], ALU.pow).then_inc(ready, 1)

            pool.wait_ge(vec, 3)
            root(nk_ss[:, 2:3], nk_ss[:, 1:2], 1, nk_pow)
            for layer in range(2):
                pool.wait_ge(z_mv, layer + 1)
                pool.tensor_tensor(ve[:], mv[:, :, 1], eps[:], ALU.add).then_inc(z_ve, 1)
                pool.wait_ge(z_ve, layer + 1)
                root(rstd[:], ve[:], T, z_rstd)

            def fill(name, i, b):
                if name == "xt":
                    pool.wait_ge(mv_ready, at(b, T, i + 1))
                    pool.tensor_tensor(ve[:, i:i + 1], mv[:, i, 1:2], eps[:, 0:1], ALU.add).then_inc(ve_made, 1)
                    pool.wait_ge(ve_made, at(b, T, i + 1))
                    root(rstd[:, i:i + 1], ve[:, i:i + 1], 1, rstd_ready)
                elif name == "kvn":
                    pool.wait_ge(kssg_made, at(b, 1, 1))
                    root(rk[:], kssg[:], T, rk_ready)
                elif name in ("q0", "q1"):
                    c = int(name[1])
                    n = at(b, 2 * T, T * c + i)
                    pool.wait_ge(qssg_made, n + 1)
                    root(rq[:], qssg[:], HC, rq_ready)
                    if c == 0 and i == 0:
                        drained(pool, b, "nn", 0)
                    pool.wait_ge(rq_ready, n + 1)
                    pool.tensor_tensor(nsq[:], nsr[:, i, c * HC:(c + 1) * HC], rq[:], ALU.mult).then_inc(nsq_made, 1)
                    pool.wait_ge(nsq_made, n + 1)
                    pool.tensor_tensor(nsn[:, i, c * HC:(c + 1) * HC], nsq[:], nb_row[:, c * HC:(c + 1) * HC],
                                       ALU.subtract).then_inc(nsn_ready, 1)
                elif name == "c":
                    pool.wait_ge(cmv_ready, at(b, T, i + 1))
                    pool.tensor_tensor(cve[:], cmv[:, 1:2], eps[:, 0:1], ALU.add).then_inc(cve_made, 1)
                    pool.wait_ge(cve_made, at(b, T, i + 1))
                    root(crs[:], cve[:], 1, crs_ready)

            def null_score(b, p, h):
                s = slot(p, h)
                pool.wait_ge(biased, at(b, 64, 8 * p + T * (h + 1)))
                pool.tensor_tensor(dn[:, s, :], nsn[:, :, 2 * p + h], mn[:, s, :], ALU.subtract).then_inc(dn_ready, 1)

            def denominator(b, p, h):
                s = slot(p, h)
                pool.wait_ge(pn_ready, at(b, H, 2 * p + h + 1))
                pool.tensor_tensor(den[:, s, :], rs[:, s, :], pn[:, s, :], ALU.add).then_inc(den_ready, 1)

            def normalise(b, p, h):
                s = slot(p, h)
                pool.wait_ge(rr_ready, at(b, H, 2 * p + h + 1))
                if p == 0 and h == 0:
                    wait(pool, pnt_ps, at(b, 1, 0))
                pool.tensor_tensor(pnat[:, :, 2 * p + h], pn[:, s, :], rr[:, s, :], ALU.mult).then_inc(pnat_ready, 1)
                for t in range(T):
                    e = pr[:, s, S_AT[t]:S_AT[t] + S_N[t]]
                    m = pool.tensor_tensor(e, e, rr[:, s, t:t + 1].broadcast_to([P, S_N[t]]), ALU.mult)
                m.then_inc(normed, 1)

            def run(b, p):
                fb, fp = following(b, p)
                for what, i in ORDER:
                    if what == "qk" and fb is not None and i % T == T - 1:
                        null_score(fb, fp, i // T)
                    elif what == "null" and fb is not None:
                        denominator(fb, fp, i)
                        normalise(fb, fp, i)
                    elif what == "fill":
                        for f in fillers(b, p, i):
                            fill(*f)

            for name, i in first_projections():
                fill(name, i, 0)
            iterations(pool, run)
            for t in range(T):
                fill("c", t, B - 1)

        @block.vector
        def _(dve):
            dve.wait_ge(id_made, 1)
            dve.tensor_copy(ident16[:], ident[:]).then_inc(id_made, 1)
            for i in range(2):
                dve.memset(qb[i][DH:DH + 1], PADK)
            dve.memset(nvw[:].bitcast(F32), 0.0).then_inc(zeros, 1)
            dve.memset(pnt[:].bitcast(F32), 0.0).then_inc(zeros, 1)
            dve.wait_ge(rows_in, ROWS_IN)
            dve.wait_ge(consts, 4)
            dve.scalar_tensor_tensor(s_row[:], s_row[:], -SCALE, ks_row[:], ALU.mult, ALU.mult).then_inc(vec, 1)
            dve.tensor_tensor_reduce(nk_sq, nk_row[:], nk_row[:], 1.0, 0.0, ALU.mult, ALU.add, nk_ss[:, 0:1]).then_inc(vec, 1)
            dve.wait_ge(vec, 2)
            dve.tensor_scalar(nk_ss[:, 1:2], nk_ss[:, 0:1], 1e-24, None, ALU.max).then_inc(vec, 1)
            dve.wait_ge(nk_pow, 1)
            dve.scalar_tensor_tensor(nk_row[:], nk_row[:], nk_ss[:, 2:3], s_row[:], ALU.mult, ALU.mult).then_inc(vec, 1)
            for h in range(2):
                dst = nv_blk[h * DH:(h + 1) * DH, :, :].rearrange("p a b -> p (a b)")[:, h:h + (H + 2) * (PAIRS - 1) + 1:H + 2]
                dve.tensor_copy(dst, nv_col[h * DH:(h + 1) * DH, :].broadcast_to([DH, PAIRS])).then_inc(vec, 1)
            dve.memset(tab[:, N:RW], MASKED).then_inc(tab_made, 1)
            dve.memset(kb[:], 0.0).then_inc(vec, 1)
            dve.wait_ge(vec, 7)

            def lo_weights(k):
                f = stage[k % 2]
                dve.wait_ge(hi_made, k + 1)
                if k < KC:
                    dve.scalar_tensor_tensor(wq_lo[:, k, :], f, g_col[:, k:k + 1], wq_hi[:, k, :].bitcast(F32),
                                             ALU.mult, ALU.subtract)
                    if k:
                        dve.wait_ge(wn_made, k)
                    dve.tensor_tensor(prod.rearrange("p (h d) -> p h d", h=H), f.rearrange("p (h d) -> p h d", h=H),
                                      nk_row[:].unsqueeze(1).broadcast_to([P, H, DH]), ALU.mult).then_inc(stage_read, 1)
                    dve.wait_ge(stage_read, k + 1)
                    dve.tensor_reduce(wn[:, k, :], prod.rearrange("p (h d) -> p h d", h=H), AX.X, ALU.add).then_inc(wn_made, 1)
                elif k == KC:
                    for j in range(KC):
                        dve.scalar_tensor_tensor(wkv_lo[:, j, 0:H], wn[:, j, :], g_col[:, j:j + 1],
                                                 wkv_hi[:, j, 0:H].bitcast(F32), ALU.mult, ALU.subtract)
                        a = dve.scalar_tensor_tensor(wkv_lo[:, j, H:], f[:, j * P:(j + 1) * P], g_col[:, j:j + 1],
                                                     wkv_hi[:, j, H:].bitcast(F32), ALU.mult, ALU.subtract)
                    a.then_inc(stage_read, 1)
                else:
                    j = k - KC - 1
                    dst = wo_lo[:, 2 * j:2 * j + 2, :].rearrange("p a n -> p (a n)")
                    hi = wo_hi[:, 2 * j:2 * j + 2, :].rearrange("p a n -> p (a n)").bitcast(F32)
                    dve.tensor_tensor(dst, f, hi, ALU.subtract).then_inc(stage_read, 1)

            for layer in range(2):
                for m in range(T):
                    if layer == 0:
                        dve.scalar_tensor_tensor(z[:, m, :], row_w0, dist[:, m:m + 1], row_b0, ALU.mult, ALU.add).then_inc(z_sum, 1)
                    else:
                        dve.wait_ge(h_mm, m + 1)
                        bank = [ps_s[0], ps_s[1], ps_pt[0], ps_pt[1]][m]
                        dve.tensor_tensor(z[:, m, :], bank[:], row_b1, ALU.add).then_inc(z_sum, 1)
                for m in range(T):
                    dve.wait_ge(z_sum, T * layer + m + 1)
                    dve.bn_stats(bn6[:, m, :], z[:, m, :]).then_inc(z_stats, 1)
                dve.wait_ge(z_stats, T * (layer + 1))
                for m in range(T):
                    a = dve.bn_aggr(mv[:, m, :], bn6[:, m, :])
                a.then_inc(z_mv, 1)
                dve.wait_ge(z_rstd, layer + 1)
                for m in range(T):
                    dve.tensor_scalar(z[:, m, :], z[:, m, :], mv[:, m, 0:1], rstd[:, m:m + 1], ALU.subtract, ALU.mult
                                      ).then_inc(z_norm, 1)
                dve.wait_ge(z_norm, T * (layer + 1))
                gain = (row_g0, row_g1)[layer].unsqueeze(1).broadcast_to([P, T, D])
                dve.tensor_tensor(z, z, gain, ALU.mult).then_inc(z_gain, 1)
                dve.wait_ge(z_exp, layer + 1)
                dve.tensor_scalar(ez, ez, 1.0, None, ALU.add).then_inc(z_step, 1)
                dve.wait_ge(z_step, 2 * layer + 1)
                dve.reciprocal(ez, ez).then_inc(z_step, 1)
                dve.wait_ge(z_step, 2 * layer + 2)
                dve.tensor_tensor(z, z, ez, ALU.mult).then_inc(z_act, 1)
                if layer == 0:
                    for k in range(KC):
                        lo_weights(k)
            dve.wait_ge(tab_ps, 1)
            dve.tensor_scalar(tab[:, 0:N], ps_o[0:H, :], b2_col[:], -1.0, ALU.add, ALU.mult).then_inc(tab_made, 1)
            for k in range(KC, 2 * KC + 1):
                lo_weights(k)
            dve.wait_ge(nvw_hi_made, 1)
            dve.tensor_tensor(nvw[Q:Q + H, :], ps_g[0][0:H, :], nvw[0:H, :].bitcast(F32), ALU.subtract).then_inc(weights, 1)

            def normalise_x(b, t):
                dve.wait_ge(x_in[t % 2], at(b, 32, 16 * (t // 2 + 1)))
                dve.bn_stats(bn6[:, t, :], xs[:, t % 2, :]).then_inc(stats, 1)
                wait_apart(stats, at(b, T, t + 1))
                dve.bn_aggr(mv[:, t, :], bn6[:, t, :]).then_inc(mv_ready, 1)
                dve.wait_ge(rstd_ready, at(b, T, t + 1))
                dve.tensor_scalar(xs[:, t % 2, :], xs[:, t % 2, :], mv[:, t, 0:1], rstd[:, t:t + 1], ALU.subtract, ALU.mult
                                  ).then_inc(xn_ready, 1)

            def keys(b, bank, done):
                rows = bank[:, :].rearrange("p (t n) -> p t n", t=T)
                dve.wait_ge(ksq_made, at(b, 1, 1))
                dve.tensor_reduce(kss[:], ksq, AX.X, ALU.add).then_inc(kss_made, 1)
                dve.tensor_copy(vst[:], rows[:, :, DH:]).then_inc(vst_made, 1)
                dve.wait_ge(kss_made, at(b, 1, 1))
                dve.tensor_scalar(kssg[:], kss[:], 1e-24, None, ALU.max).then_inc(kssg_made, 1)
                dve.wait_ge(rk_ready, at(b, 1, 1))
                for t in range(T):
                    a = dve.scalar_tensor_tensor(kh[:, t, :], rows[:, t, 0:DH], rk[:, t:t + 1], s_row[:], ALU.mult, ALU.mult)
                a.then_inc(done, 1)
                drained(dve, b, "kvn", 0)
                wait(dve, kt_ps, at(b, 1, 0))
                hi = knat[:, :, 0:2 * DH].rearrange("p t (a d) -> p t a d", a=2)
                dve.tensor_copy(hi, kh.unsqueeze(2).broadcast_to([P, T, 2, DH])).then_inc(khi_made, 1)
                dve.wait_ge(khi_made, at(b, 1, 1))
                dve.tensor_tensor(knat[:, :, 2 * DH:], kh, knat[:, :, 0:DH], ALU.subtract).then_inc(kn_ready, 1)

            def settle_kv(b):
                bank, done = bank_of(b, "kt", 0)
                f16 = bank[:, :].bitcast(F16)
                dve.wait_ge(kt_ps, at(b, 1, 1))
                dve.tensor_copy(ka[:], f16[:, 0:N])
                dve.tensor_copy(kb[0:DH, :], f16[0:DH, N:]).then_inc(done, 1)
                dve.wait_ge(mask_in, at(b, 16, 16))
                dve.tensor_scalar(kb[DH:DH + 1, :], mask_u8[DH:DH + 1, :], -PADK, PADK, ALU.mult, ALU.add).then_inc(kv_ready, 1)

            def settle_v(b):
                wait(dve, pv_done, at(b, 3 * PAIRS, 0))
                dve.wait_ge(vst_made, at(b, 1, 1))
                dve.tensor_copy(v[:], vst[:]).then_inc(v_ready, 1)

            def split_q(b, c, i):
                n = at(b, 2 * T, T * c + i)
                bank, done = bank_of(b, f"q{c}", i)
                dve.wait_ge(qsq_made, n + 1)
                wait(dve, rq_ready, n)
                dve.tensor_reduce(qss[:], qsq[:], AX.X, ALU.add).then_inc(qss_made, 1)
                dve.wait_ge(qss_made, n + 1)
                dve.tensor_scalar(qssg[:], qss[:], 1e-24, None, ALU.max).then_inc(qssg_made, 1)
                dve.wait_ge(rq_ready, n + 1)
                dve.tensor_tensor(qf[:], bank[:, :].rearrange("p (h d) -> p h d", h=HC),
                                  rq[:].unsqueeze(2).broadcast_to([P, HC, DH]), ALU.mult).then_inc(done, 1)
                drained(dve, b, f"q{c}", i)
                dve.tensor_copy(qn[c][:, i, :, 0:DH], qf[:]).then_inc(qhi_made, 1)
                dve.wait_ge(qhi_made, n + 1)
                dve.tensor_tensor(qn[c][:, i, :, DH:], qf[:], qn[c][:, i, :, 0:DH], ALU.subtract).then_inc(qn_ready, 1)

            def finish_rows(b, t):
                bank, done = bank_of(b, "c", t)
                dve.wait_ge(c_ps, at(b, T, t + 1))
                dve.bn_stats(cbn6[:], bank[:]).then_inc(cstats, 1)
                wait_apart(cstats, at(b, T, t + 1))
                dve.bn_aggr(cmv[:], cbn6[:]).then_inc(cmv_ready, 1)
                dve.wait_ge(cmv_ready, at(b, T, t + 1))
                dve.scalar_tensor_tensor(bank[:], bank[:], cmv[:, 0:1], gout_row[:], ALU.subtract, ALU.mult).then_inc(og_made, 1)
                dve.wait_ge(og_made, at(b, T, t + 1))
                dve.wait_ge(crs_ready, at(b, T, t + 1))
                dve.wait_ge(res_in[t % 2], at(b, 16 * (T // 2), 16 * (t // 2 + 1)))
                dve.scalar_tensor_tensor(res[t % 2][:], bank[:], crs[:], res[t % 2][:], ALU.mult, ALU.add).then_inc(done, 1)

            def fill(name, i, b):
                bank, done = bank_of(b, name, i)
                if name == "xt":
                    normalise_x(b, i)
                    dve.wait_ge(xt_hi_made, at(b, T, i + 1))
                    dst, hi = (a[:, :, i * P:(i + 1) * P] for a in (xt_lo, xt_hi))
                    dve.tensor_tensor(dst, bank[:, :].rearrange("p (k n) -> p k n", k=KC), hi.bitcast(F32),
                                      ALU.subtract).then_inc(done, 1)
                elif name == "kvn":
                    keys(b, bank, done)
                elif name == "nn":
                    dve.wait_ge(nn_ps, at(b, 1, 1))
                    wait(dve, nsn_ready, at(b, 2 * T, 0))
                    dve.tensor_copy(nsr[:], bank[:, 0:T * H].rearrange("p (t h) -> p t h", t=T)).then_inc(done, 1)
                elif name in ("q0", "q1"):
                    split_q(b, int(name[1]), i)
                elif name == "pnt":
                    dve.wait_ge(pnh_made, at(b, 1, 1))
                    dve.tensor_tensor(pnt[2 * Q:2 * Q + H, :], bank[0:H, :], pnt[0:H, :].bitcast(F32), ALU.subtract).then_inc(done, 1)
                elif name == "c":
                    finish_rows(b, i)

            def add_bias(b, p, i):
                h, t = TILE_OF[i]
                s = slot(p, h)
                if i == 0:
                    dve.wait_ge(tb_in[p % 2], at(b, 16 * PAIRS // 2, 16 * (p // 2 + 1)))
                    dve.wait_ge(nsn_ready, at(b, 2 * T, T * (p // (HC // 2)) + T))
                    wait(dve, pt_ps, at(b, GROUPS * PAIRS, GROUPS * (p - 1)))
                    wait(dve, dn_ready, at(b, H, 2 * p - 2))
                wait_apart(qk_ps, at(b, 64, 8 * p + i + 1))
                off = (T - 1 - t) * P
                dve.tensor_tensor_reduce(pr[:, s, S_AT[t]:S_AT[t] + S_N[t]], ps_s[i % 2][:, 0:S_N[t]],
                                         tb[p % 2][:, h, off:off + S_N[t]], 1.0, nsn[:, t, 2 * p + h:2 * p + h + 1],
                                         ALU.add, ALU.min, mn[:, s, t:t + 1]).then_inc(biased, 1)

            def invert(b, p, h):
                s = slot(p, h)
                dve.wait_ge(den_ready, at(b, H, 2 * p + h + 1))
                dve.reciprocal(rr[:, s, :], den[:, s, :]).then_inc(rr_ready, 1)

            def run(b, p):
                fb, fp = following(b, p)
                for what, i in ORDER:
                    if what == "qt" and fb is not None:
                        if fp == 0:
                            settle_kv(fb)
                        dve.wait_ge(qt_ps, at(fb, PAIRS, fp + 1))
                        dve.tensor_copy(qa[fp % 2][:], ps_qt[:]).then_inc(qa_ready, 1)
                    elif what == "qk" and fb is not None:
                        add_bias(fb, fp, i)
                    elif what == "null" and fb is not None:
                        invert(fb, fp, i)
                    elif what == "fill":
                        for f in fillers(b, p, i):
                            fill(*f)
                    elif what == "pt" and p >= 0 and (GROUPS * p + i) % 2 == 1:
                        n = GROUPS * p + i
                        dve.wait_ge(pt_ps, at(b, GROUPS * PAIRS, n + 1))
                        wait(dve, pv_done, at(b, 3 * PAIRS, slot_free(n)))
                        dve.tensor_copy(pts[:, n % PSLOTS, :], ps_pt[1][:]).then_inc(pt_drained[1], 1)
                    elif what == "pv" and i == 0 and p == 0:
                        pass
                    elif what == "pv" and i == 2 and p >= 0:
                        dve.wait_ge(oh_made, at(b, PAIRS, p + 1))
                        dve.tensor_tensor(ot_lo[:, p, :], ps_o[:], ot_hi[:, p, :].bitcast(F32), ALU.subtract).then_inc(o_drained, 1)
                if p == -1 or (p == PAIRS - 1 and fb is not None):
                    settle_v(fb)

            for name, i in first_projections():
                fill(name, i, 0)
            iterations(dve, run)
            for t in range(T):
                fill("c", t, B - 1)


ROWS_IN = 16 * 15
_INS = ["x", "cond_64", "mask_BxS_bf1", "L0_cond_g_norm", "L0_cond_Wq", "L0_cond_Wkv", "L0_cond_q_scale",
        "L0_cond_k_scale", "L0_cond_null_attn_bias", "L0_cond_w0", "L0_cond_b0", "L0_cond_g0", "L0_cond_w1",
        "L0_cond_b1", "L0_cond_g1", "L0_cond_w2", "L0_cond_b2", "L0_cond_Wout", "L0_cond_g_out"]


def kernel(**inputs):
    import numpy as _np
    import concourse.bacc as _bacc
    from concourse import mybir as _mybir
    from concourse.bass_utils import run_bass_kernel_spmd as _run

    nc = _bacc.Bacc("TRN2", target_bir_lowering=False, num_devices=1)
    arrays, args = {}, []
    for name in _INS:
        a = _np.ascontiguousarray(inputs[name])
        if a.dtype == _np.bool_:
            a = a.view(_np.uint8)
        arrays[name] = a
        args.append(nc.dram_tensor(name, a.shape, _mybir.dt.from_np(a.dtype), kind="ExternalInput").ap())
    out = nc.dram_tensor("out", (B, N, D), _mybir.dt.float32, kind="ExternalOutput").ap()
    build(nc, *args, out)
    r = _run(nc, [arrays], core_ids=[0])
    return r.results[0]["out"]
```

```python
import numpy as np
import concourse.bass as bass
from concourse import mybir
from contextlib import ExitStack

B, N, D = 8, 512, 512
H, DH = 16, 64
P = 128
Q = 32
T = N // P
KC = D // P
PAIRS = H // 2
CH = 2
HC = H // CH
SCALE = 8.0
EPS = 1e-5
MASKED = 1e30
PADK = 32768.0
RW = N + P
HEADSLOTS = 4
GROUPS = 5
PSLOTS = 4
S_AT = [P * t * (t + 1) // 2 for t in range(T)]
S_N = [P * (t + 1) for t in range(T)]
S_ALL = sum(S_N)
GROUP = [[(0, 0, 0)], [(0, 1, 0), (0, 3, 384)], [(1, 0, 0)], [(1, 1, 0), (1, 3, 384)], [(0, 2, 0), (1, 2, 256)]]
PV_SETS = [[(0, ((0, 0), (2, 0)))], [(1, ((1, 0), (3, 0))), (3, ((1, 384), (3, 384)))], [(2, ((4, 0), (4, 256)))]]
PV_NEEDS = [2, 3, 4]
PV_FREES = {0: 0, 2: 0, 1: 1, 3: 1, 4: 2}
ORDER = [("qk", 0), ("qk", 1), ("fill", 0), ("qk", 2), ("pt", 0), ("qk", 3), ("pt", 1), ("qk", 4),
         ("fill", 1), ("qk", 5), ("pt", 2), ("qk", 6), ("pt", 3), ("qk", 7), ("qt", 0),
         ("fill", 2), ("pt", 4), ("pv", 0), ("pv", 1), ("pv", 2)]
STEPS = len(ORDER)
TILE_OF = [(0, 3), (0, 2), (0, 1), (0, 0), (1, 3), (1, 2), (1, 1), (1, 0)]
FILL = {
    0: [[("c", 0, -1)], [("c", 1, -1)], [("c", 2, -1), ("c", 3, -1)]],
    1: [[("q1", 1, 0)], [("q1", 2, 0)], []],
    2: [[("q1", 3, 0)], [], []],
    3: [[("xt", 0, 1), ("xt", 1, 1)], [], [("xt", 2, 1), ("xt", 3, 1)]],
    4: [[("nul", 0, 1), ("kv", 0, 1)], [("nn", 0, 1), ("q0", 0, 1)], []],
    5: [[("kvn", 0, 1), ("q0", 1, 1)], [("q0", 2, 1)], []],
    6: [[("q0", 3, 1)], [], []],
    7: [[], [("pnt", 0, 0)], [("q1", 0, 1)]],
}
DVE_STAGES = {"xt": [-12, -5, 1], "kvn": [1, 4], "nn": [1], "q0": [1, 5], "q1": [1, 5], "pnt": [1], "c": [1, 2]}
ACT_STAGES = {"xt": [0], "kv": [0], "nul": [0], "kvn": [0], "q0": [0], "q1": [0], "pnt": [0]}
POOL_STAGES = {"xt": [-11], "kvn": [2], "q0": [2, 5], "q1": [2, 5], "c": [1]}
DN_AT, PN_AT, DEN_AT, RR_AT = [5, 13], [7, 15], [7, 15], [9, 16]
PT_BY_DVE = (1,)


def exists(b):
    return not isinstance(b, int) or 0 <= b < B


def is_first(b):
    return isinstance(b, int) and b == 0


def pair(b, p):
    if p >= PAIRS:
        b, p = b + 1, p - PAIRS
    return (b, p) if exists(b) else (None, None)


def fillers(b, p, k):
    if p < 0:
        b, p = b - 1, p + PAIRS
    if p >= PAIRS:
        b, p = b + 1, p - PAIRS
    for name, i, offset in FILL[p][k]:
        if exists(b + offset):
            yield name, i, b + offset


def stages(lags, b, p, step):
    for d in (-1, 0, 1):
        for k in range(3):
            for name, i, batch in fillers(b, p + d, k):
                for s, lag in enumerate(lags.get(name, ())):
                    if ORDER.index(("fill", k)) + lag + d * STEPS == step:
                        yield name, i, batch, s


def iterations(eng, run):
    def batch(b):
        for p in range(1, PAIRS):
            run(b, p)

    for p in range(2, PAIRS):
        run(-1, p)
    run(0, 0)
    batch(0)
    run(1, 0)
    with eng.Fori(1, B - 1) as b:
        batch(b)
        run(b + 1, 0)
    batch(B - 1)
    run(B, 0)


def at(b, per, n):
    return b * per + n


def wait(eng, sem, value):
    if isinstance(value, int) and value <= 0:
        return
    eng.wait_ge(sem, value)


def general_uses():
    uses = {}
    for b in range(-1, B + 1):
        for p in range(PAIRS):
            for what, k in ORDER:
                if what == "fill":
                    for name, i, batch in fillers(b, p, k):
                        uses[batch, name, i] = len(uses)
                elif what == "qt" and pair(b, p + 2)[1] == 0:
                    uses[pair(b, p + 2)[0], "kt", 0] = len(uses)
    return uses


G_USES = general_uses()
G_PER = G_USES[3, "c", 0] - G_USES[2, "c", 0]


def g_use(b, name, i):
    if isinstance(b, int):
        k = G_USES[b, name, i]
        return k % 2, k // 2
    k = G_USES[2, name, i] - 2 * G_PER
    return k % 2, b * (G_PER // 2) + k // 2


def build(nc, x, cond, mask, g_norm, Wq, Wkv, q_scale, k_scale, null_bias,
          w0, b0, g0, w1, b1, g1, w2, b2, Wout, g_out, out):
    F32, F32R, F16, U8 = mybir.dt.float32, mybir.dt.float32r, mybir.dt.float16, mybir.dt.uint8
    ALU, ACT, AX = mybir.AluOpType, mybir.ActivationFunctionType, mybir.AxisListType

    table = nc.dram_tensor("bias_table", (H, P * RW), F32).ap()

    ctx = ExitStack()
    with ctx:
        def sb(name, shape, dt=F32):
            return ctx.enter_context(nc.sbuf_tensor(name, shape, dt))

        def pb(name, shape, dt=F32):
            return ctx.enter_context(nc.psum_tensor(name, shape, dt))

        def sem(name):
            return ctx.enter_context(nc.semaphore(name))

        wq_hi = sb("wq_hi", [P, KC, H * DH], F32R)
        wq_lo = sb("wq_lo", [P, KC, H * DH], F32R)
        wkv_hi = sb("wkv_hi", [P, KC, H + 2 * DH], F32R)
        wkv_lo = sb("wkv_lo", [P, KC, H + 2 * DH], F32R)
        wo_hi = sb("wo_hi", [P, PAIRS, D], F32R)
        wo_lo = sb("wo_lo", [P, PAIRS, D], F32R)
        nvw = sb("nvw", [3 * Q, D], F32R)
        ident = sb("ident", [P, P])
        ident16 = sb("ident16", [P, P], F16)
        half = sb("half", [P, H])
        eps = sb("eps", [P, T])
        g_col = sb("g_col", [P, KC])
        gout_row = sb("gout_row", [P, D])
        nb_row = sb("nb_row", [P, H])
        s_row = sb("s_row", [P, DH])
        nk_row = sb("nk_row", [P, DH])
        ks_row = sb("ks_row", [P, DH])
        xs = sb("xs", [P, 2, D])
        xt_hi = sb("xt_hi", [P, KC, N], F32R)
        xt_lo = sb("xt_lo", [P, KC, N], F32R)
        bn6 = sb("bn6", [P, T, 6])
        mv = sb("mv", [P, T, 2])
        ve = sb("ve", [P, T])
        rstd = sb("rstd", [P, T])
        kvt = xs[:, 0, :]
        nt = sb("nt", [H, RW])
        kss = sb("kss", [P, T])
        kssg = sb("kssg", [P, T])
        rk = sb("rk", [P, T])
        knat = sb("knat", [P, T, 3 * DH], F16)
        vst = sb("vst", [P, T, DH])
        v = sb("v", [P, T, DH])
        ka = sb("ka", [P, N], F16)
        kb = sb("kb", [P, N], F16)
        mask_u8 = sb("mask_u8", [P, N], U8)
        nsr = sb("nsr", [P, T, H])
        qsq = sb("qsq", [P, HC, DH])
        qss = sb("qss", [P, HC])
        qssg = sb("qssg", [P, 2, HC])
        rq = sb("rq", [P, 2, HC])
        nsq = sb("nsq", [P, HC])
        qf = sb("qf", [P, HC, DH])
        ksq, kh = qsq[:, 0:T, :], qf[:, 0:T, :]
        qn = [sb(f"qn{c}", [P, T, HC, 2 * DH], F16) for c in range(CH)]
        nsn = sb("nsn", [P, T, H])
        qa = [sb(f"qa{i}", [P, 2, N], F16) for i in range(2)]
        qb = [sb(f"qb{i}", [DH + 1, 2, N], F16) for i in range(2)]
        tb = [sb(f"tb{i}", [P, 2, N]) for i in range(2)]
        pr = sb("pr", [P, HEADSLOTS, S_ALL])
        mn = sb("mn", [P, HEADSLOTS, T])
        rs = sb("rs", [P, HEADSLOTS, T])
        dn = sb("dn", [P, HEADSLOTS, T])
        pn = sb("pn", [P, HEADSLOTS, T])
        den = sb("den", [P, HEADSLOTS, T])
        rr = sb("rr", [P, HEADSLOTS, T])
        pnat = sb("pnat", [P, T, H])
        pts = sb("pts", [P, PSLOTS, N])
        ot_hi = sb("ot_hi", [P, PAIRS, N], F32R)
        ot_lo = sb("ot_lo", [P, PAIRS, N], F32R)
        pnt = sb("pnt", [3 * Q, N], F32R)
        cbn6 = sb("cbn6", [P, 6])
        cmv = sb("cmv", [P, 2, 2])
        cve = sb("cve", [P, 2, 1])
        crs = sb("crs", [P, 2, 1])
        res = [sb(f"res{i}", [P, D]) for i in range(2)]

        ps_s = [pb(f"ps_s{i}", [P, N]) for i in range(2)]
        ps_pt = [pb(f"ps_pt{i}", [P, N]) for i in range(2)]
        ps_o = pb("ps_o", [P, N])
        ps_g = [pb(f"ps_g{i}", [P, N]) for i in range(2)]
        ps_qt = pb("ps_qt", [P, 2, N], F16)

        z = pr[:, :, :].rearrange("p a b -> p (a b)")[:, 0:T * D].rearrange("p (t d) -> p t d", t=T)
        ez = pr[:, :, :].rearrange("p a b -> p (a b)")[:, T * D:2 * T * D].rearrange("p (t d) -> p t d", t=T)
        row_w0, row_b0, row_g0, row_b1 = (tb[i // 2][:, i % 2, :] for i in range(4))
        row_g1 = res[0][:, :]
        w1_sb = qn[0][:, :, :, :].rearrange("p a b c -> p (a b c)").bitcast(F32).rearrange("p (k n) -> p k n", k=KC)
        ht = qn[1][:, :, :, :].rearrange("p a b c -> p (a b c)").bitcast(F32).rearrange("p (k n) -> p k n", k=KC)
        stage = [pts[:, 2 * i:2 * i + 2, :].rearrange("p a b -> p (a b)") for i in range(2)]
        prod = xs[:, :, :].rearrange("p a b -> p (a b)")
        w2_sb = vst[:, 0, :].rearrange("p (k h) -> p k h", k=KC)
        wn = vst[:, 1, :].rearrange("p (k h) -> p k h", k=KC)
        nv_blk = vst[:, 2:4, :].rearrange("p a (q h) -> p (a q) h", h=H)
        b2_col = sb("b2_col", [H, 1])
        nv_col = sb("nv_col", [P, 1])
        tab = nt
        dist = sb("dist", [P, T])
        nk_sq = qsq[:, 0, :]
        nk_ss = sb("nk_ss", [P, 3])

        consts = sem("consts"); id_zero = sem("id_zero"); id_made = sem("id_made")
        rows_in = sem("rows_in"); w1_in = sem("w1_in")
        stage_in = [sem("stage_in0"), sem("stage_in1")]
        hi_made = sem("hi_made"); stage_read = sem("stage_read"); nvw_acc = sem("nvw_acc")
        vec = sem("vec"); nk_pow = sem("nk_pow"); wn_made = sem("wn_made")
        nvw_hi_made = sem("nvw_hi_made"); zeros = sem("zeros"); weights = sem("weights")
        z_sum = sem("z_sum"); z_stats = sem("z_stats"); z_mv = sem("z_mv"); z_ve = sem("z_ve"); z_rstd = sem("z_rstd")
        z_norm = sem("z_norm"); z_gain = sem("z_gain"); z_exp = sem("z_exp"); z_step = sem("z_step"); z_act = sem("z_act")
        h_turned = sem("h_turned"); h_drained = sem("h_drained"); h_mm = sem("h_mm"); tab_ps = sem("tab_ps"); tab_made = sem("tab_made")
        tab_out = sem("tab_out")
        passed = sem("passed")
        x_in = [sem("x_in0"), sem("x_in1")]; stats = sem("stats"); mv_ready = sem("mv_ready"); ve_made = sem("ve_made"); rstd_ready = sem("rstd_ready")
        xn_ready = sem("xn_ready"); xt_ps = sem("xt_ps"); xt_hi_made = sem("xt_hi_made")
        kv_ps = sem("kv_ps"); nul_ps = sem("nul_ps"); kvn_ps = sem("kvn_ps"); nn_ps = sem("nn_ps")
        ksq_made = sem("ksq_made"); kss_made = sem("kss_made"); kssg_made = sem("kssg_made"); rk_ready = sem("rk_ready")
        khi_made = sem("khi_made"); kn_ready = sem("kn_ready"); kt_ps = sem("kt_ps"); mask_in = sem("mask_in")
        kv_ready = sem("kv_ready"); v_ready = sem("v_ready"); vst_made = sem("vst_made")
        q_ps = sem("q_ps"); qsq_made = sem("qsq_made"); qss_made = sem("qss_made"); qssg_made = sem("qssg_made"); rq_ready = sem("rq_ready")
        nsq_made = sem("nsq_made"); nsn_ready = sem("nsn_ready"); qhi_made = sem("qhi_made"); qn_ready = sem("qn_ready")
        g_drained = [sem("g_drained0"), sem("g_drained1")]
        qt_ps = sem("qt_ps"); qa_ready = sem("qa_ready"); qb_ready = sem("qb_ready")
        tb_in = [sem("tb_in0"), sem("tb_in1")]
        qk_ps = sem("qk_ps"); biased = sem("biased"); exp_done = sem("exp_done")
        dn_ready = sem("dn_ready"); pn_ready = sem("pn_ready"); den_ready = sem("den_ready"); rr_ready = sem("rr_ready")
        normed = sem("normed"); pnat_ready = sem("pnat_ready"); pt_ps = sem("pt_ps"); pt_drained = [sem("pt_drained0"), sem("pt_drained1")]
        pv_done = sem("pv_done"); oh_made = sem("oh_made"); o_drained = sem("o_drained")
        pnt_ps = sem("pnt_ps"); pnh_made = sem("pnh_made"); c_ps = sem("c_ps"); cstats = sem("cstats")
        cmv_ready = sem("cmv_ready"); cve_made = sem("cve_made"); crs_ready = sem("crs_ready"); og_made = sem("og_made")
        res_in = [sem("res_in0"), sem("res_in1")]; out_sent = [sem("out_sent0"), sem("out_sent1")]

        def slot(p, h):
            return (2 * p + h) % HEADSLOTS

        def slot_free(n):
            p, g = divmod(n - PSLOTS, GROUPS)
            return 3 * p + PV_FREES[g] + 1

        def wait_apart(sem, value):
            nc.vector.wait_ge(sem, value)
            nc.vector.sem_inc(passed, 1)

        def drained(eng, b, name, i):
            bank, before = g_use(b, name, i)
            eng.wait_ge(g_drained[bank], before + 1)

        def claim(eng, b, name, i):
            bank, before = g_use(b, name, i)
            wait(eng, g_drained[bank], before)
            return ps_g[bank]

        def bank_of(b, name, i):
            return ps_g[g_use(b, name, i)[0]], g_drained[g_use(b, name, i)[0]]

        block = ctx.enter_context(nc.Block())

        @block.sync
        def _(sp):
            def load_x(b, tiles):
                for t in tiles:
                    wait(sp, weights, 0 if is_first(b) else 1)
                    wait(sp, xt_ps, at(b, T, t - 1))
                    if t == 0:
                        wait(sp, kvn_ps, at(b, 1, 0))
                    sp.dma_start(xs[:, t % 2, :], x[bass.ds(b, 1), t * P:(t + 1) * P, :].rearrange("a p d -> (a p) d")
                                 ).then_inc(x_in[t % 2], 16)

            for dst, src in ((row_w0, w0[0, :]), (row_b0, b0), (row_g0, g0), (row_b1, b1), (row_g1, g1),
                             (nk_row[:], cond[0, :]), (s_row[:], q_scale), (ks_row[:], k_scale),
                             (nb_row[:], null_bias), (gout_row[:], g_out)):
                sp.dma_start(dst, src.partition_broadcast(P)).then_inc(rows_in, 16)
            sp.dma_start(w2_sb, w2.rearrange("(k p) h -> p k h", p=P)).then_inc(rows_in, 16)
            sp.dma_start(b2_col[:], b2.unsqueeze(1)).then_inc(rows_in, 16)
            sp.dma_start(g_col[:], g_norm.rearrange("(k p) -> p k", p=P),
                         allow_slow_non_contiguous=True).then_inc(rows_in, 16)
            for h in range(2):
                sp.dma_start(nv_col[h * DH:(h + 1) * DH, :], cond[1, :].unsqueeze(1)).then_inc(rows_in, 16)
            sp.dma_start(w1_sb, w1.rearrange("(k p) n -> p k n", p=P)).then_inc(w1_in, 16)
            for k in range(2 * KC + 1):
                wait(sp, stage_read, k - 1)
                wait(sp, nvw_acc, k - 2 - KC)
                if k < KC:
                    dst, src = stage[k % 2], Wq[k * P:(k + 1) * P, :]
                elif k == KC:
                    dst = stage[0][:, 0:KC * 2 * DH].rearrange("p (k n) -> p k n", k=KC)
                    src = Wkv.rearrange("(k p) n -> p k n", p=P)
                else:
                    j = k - KC - 1
                    dst = stage[k % 2].rearrange("p (a n) -> p a n", a=2)
                    src = Wout[2 * j * P:2 * (j + 1) * P, :].rearrange("(a p) n -> p a n", p=P)
                sp.dma_start(dst, src).then_inc(stage_in[k % 2], 16)
            sp.wait_ge(tab_made, 2)
            for h in range(H):
                sp.dma_start(table[h:h + 1, :].rearrange("a (p u) -> a p u", p=P),
                             tab[h:h + 1, :].unsqueeze(1).broadcast_to([1, P, RW])).then_inc(tab_out, 16)
            sp.wait_ge(tab_out, 16 * H)
            sp.wait_ge(wn_made, KC)
            load_x(0, (0, 1))
            sp.dma_start(mask_u8[DH:DH + 1, :], mask[0:1, :]).then_inc(mask_in, 16)

            def load_bias(b, p):
                wait(sp, weights, 0 if is_first(b) else 1)
                wait(sp, biased, at(b, 64, 8 * (p - 1)))
                src = bass.AP(table.tensor, 2 * p * P * RW + P - 1, [[RW - 1, P], [P * RW, 2], [1, N]])
                sp.dma_start(tb[p % 2][:], src).then_inc(tb_in[p % 2], 16)

            def store(b):
                for t in range(2):
                    load_rows(b, t)
                for t in range(T):
                    sp.wait_ge(weights, 1)
                    drained(sp, b, "c", t)
                    sp.dma_start(out[bass.ds(b, 1), t * P:(t + 1) * P, :].rearrange("a p d -> (a p) d"), res[t % 2][:]
                                 ).then_inc(out_sent[t % 2], 16)
                    if t + 2 < T:
                        load_rows(b, t + 2)

            def load_rows(b, t):
                    sp.wait_ge(weights, 1)
                    wait(sp, out_sent[t % 2], at(b, 16 * (T // 2), 16 * (t // 2)))
                    sp.dma_start(res[t % 2][:], x[bass.ds(b, 1), t * P:(t + 1) * P, :].rearrange("a p d -> (a p) d")
                                 ).then_inc(res_in[t % 2], 16)

            def run(b, p):
                nb, np_ = pair(b, p + 2)
                if nb is not None:
                    load_bias(nb, np_)
                if p == 0 and exists(b - 1):
                    store(b - 1)
                if p == 1 and exists(b + 1):
                    load_x(b + 1, (0, 1))
                    sp.wait_ge(weights, 1)
                    sp.wait_ge(kv_ready, at(b, 1, 1))
                    sp.dma_start(mask_u8[DH:DH + 1, :], mask[bass.ds(b + 1, 1), :]).then_inc(mask_in, 16)
                if p == 3 and exists(b + 1):
                    load_x(b + 1, (2, 3))

            iterations(sp, run)
            for i in range(2):
                sp.wait_ge(out_sent[i], 16 * (T // 2) * B)

        @block.tensor
        def _(pe):
            pe.wait_ge(consts, 4)
            pe.wait_ge(id_made, 2)
            banks = [ps_s[0], ps_s[1], ps_pt[0], ps_pt[1]]
            for layer in range(2):
                pe.wait_ge(z_act, layer + 1)
                for m in range(T):
                    for k in range(KC):
                        mm = pe.transpose(banks[m][:, k * P:(k + 1) * P], z[:, m, k * P:(k + 1) * P], ident[:])
                    mm.then_inc(h_turned, 1)
                pe.wait_ge(h_drained, T * (layer + 1))
                if layer == 0:
                    pe.wait_ge(w1_in, 16)
                    for m in range(T):
                        for k in range(KC):
                            mm = pe.matmul(banks[m][:], ht[:, k, m * P:(m + 1) * P], w1_sb[:, k, :],
                                           start=k == 0, stop=k == KC - 1)
                        mm.then_inc(h_mm, 1)
                else:
                    pe.wait_ge(rows_in, ROWS_IN)
                    for k in range(KC):
                        mm = pe.matmul(ps_o[0:H, :], w2_sb[:, k, :], ht[:, k, :], start=k == 0, stop=k == KC - 1)
                    mm.then_inc(tab_ps, 1)
            pe.wait_ge(vec, 7)
            for j in range(PAIRS // 2):
                k = KC + 1 + j
                pe.wait_ge(stage_in[k % 2], 16 * (k // 2 + 1))
                for a in range(2):
                    q = 2 * j + a
                    mm = pe.matmul(ps_g[0][0:H, :], nv_blk[:, q, :], stage[k % 2][:, a * D:(a + 1) * D],
                                   start=q == 0, stop=q == PAIRS - 1)
                mm.then_inc(nvw_acc, 1)
            pe.wait_ge(weights, 1)

            def turn_x(b, t):
                bank = claim(pe, b, "xt", t)
                pe.wait_ge(xn_ready, at(b, T, t + 1))
                for k in range(KC):
                    mm = pe.transpose(bank[:, k * P:(k + 1) * P], xs[:, t % 2, k * P:(k + 1) * P], ident[:])
                mm.then_inc(xt_ps, 1)

            def products(bank, pairs):
                for i, (lhs, rhs) in enumerate(pairs):
                    mm = pe.matmul(bank, lhs, rhs, start=i == 0, stop=i == len(pairs) - 1)
                return mm

            def keys_values(b, name, done, col):
                bank = claim(pe, b, name, 0)
                for t in range(T):
                    drained(pe, b, "xt", t)
                cols = slice(col, col + P)
                products(bank[:], [(w[:, k, cols], xt[:, k, :]) for k in range(KC)
                                   for w, xt in ((wkv_hi, xt_hi), (wkv_lo, xt_hi), (wkv_hi, xt_lo))]).then_inc(done, 1)

            def turn_kv(b):
                bank = claim(pe, b, "kvn", 0)
                drained(pe, b, "kv", 0)
                for t in range(T):
                    mm = pe.transpose(bank[:, t * P:(t + 1) * P], kvt[:, t * P:(t + 1) * P], ident[:])
                mm.then_inc(kvn_ps, 1)

            def turn_null(b):
                bank = claim(pe, b, "nn", 0)
                drained(pe, b, "nul", 0)
                pe.transpose(bank[:, P:2 * P], ident[:], ident[:])
                for t in range(T):
                    mm = pe.transpose(bank[:, t * H:(t + 1) * H], nt[:, t * P:(t + 1) * P], ident[0:H, 0:H])
                mm.then_inc(nn_ps, 1)

            def turn_k(b):
                bank = claim(pe, b, "kt", 0)[:, :].bitcast(F16)
                pe.wait_ge(kn_ready, at(b, 1, 1))
                for t in range(T):
                    pe.transpose(bank[:, t * P:(t + 1) * P], knat[:, t, 0:2 * DH], ident16[:])
                for t in range(T):
                    mm = pe.transpose(bank[0:DH, N + t * P:N + (t + 1) * P], knat[:, t, 2 * DH:3 * DH], ident16[:])
                mm.then_inc(kt_ps, 1)

            def project_q(b, c, t):
                bank = claim(pe, b, f"q{c}", t)
                if c == 0 and t == 0:
                    for i in range(T):
                        drained(pe, b, "xt", i)
                rows, cols = slice(t * P, (t + 1) * P), slice(c * HC * DH, (c + 1) * HC * DH)
                products(bank[:], [(xt[:, k, rows], w[:, k, cols]) for k in range(KC)
                                   for xt, w in ((xt_hi, wq_hi), (xt_hi, wq_lo), (xt_lo, wq_hi))]).then_inc(q_ps, 1)

            def turn_q(b, p):
                c, h = p // (HC // 2), 2 * (p % (HC // 2))
                pe.wait_ge(qn_ready, at(b, 2 * T, T * c + T))
                wait(pe, qb_ready, at(b, PAIRS, p))
                for i in range(2):
                    for t in range(T):
                        mm = pe.transpose(ps_qt[:, i, t * P:(t + 1) * P], qn[c][:, t, h + i, :], ident16[:])
                mm.then_inc(qt_ps, 1)

            def scores(b, p, i):
                h, t = TILE_OF[i]
                if i == 0:
                    pe.wait_ge(qb_ready, at(b, PAIRS, p + 1))
                    pe.wait_ge(kv_ready, at(b, 1, 1))
                wait(pe, biased, at(b, 64, 8 * p + i - 1))
                o = ps_s[i % 2][:, 0:S_N[t]]
                rows = slice(t * P, (t + 1) * P)
                pe.matmul(o, qa[p % 2][:, h, rows], ka[:, 0:S_N[t]], start=True, stop=False)
                pe.matmul(o, qb[p % 2][:, h, rows], kb[0:DH + 1, 0:S_N[t]], start=False, stop=True).then_inc(qk_ps, 1)

            def turn_probs(b, p, g):
                n = GROUPS * p + g
                pe.wait_ge(normed, at(b, H, 2 * p + 1 + max(h for h, _, _ in GROUP[g])))
                wait(pe, pt_drained[n % 2], at(b, 20, n // 2))
                for h, kb_, col in GROUP[g]:
                    for t in range(kb_, T):
                        at_ = S_AT[t] + kb_ * P
                        mm = pe.transpose(ps_pt[n % 2][:, col + (t - kb_) * P:col + (t - kb_ + 1) * P],
                                          pr[:, slot(p, h), at_:at_ + P], ident[:])
                mm.then_inc(pt_ps, 1)

            def weigh_values(b, p, s):
                n = GROUPS * p + PV_NEEDS[s]
                for m in range(max(0, n - 1), n + 1):
                    pe.wait_ge(pt_drained[m % 2], at(b, 20, m // 2 + 1))
                if s == 0:
                    wait(pe, o_drained, at(b, PAIRS, p))
                    if p == 0:
                        pe.wait_ge(v_ready, at(b, 1, 1))
                for kb_, places in PV_SETS[s]:
                    for h, (g, col) in enumerate(places):
                        w = (T - kb_) * P
                        mm = pe.matmul(ps_o[h * DH:(h + 1) * DH, kb_ * P:N], v[:, kb_, :], pts[:, (GROUPS * p + g) % PSLOTS, col:col + w],
                                       start=kb_ == 0, stop=kb_ == 2)
                mm.then_inc(pv_done, 1)

            def turn_null_probs(b):
                bank = claim(pe, b, "pnt", 0)
                pe.wait_ge(pnat_ready, at(b, H, H))
                for t in range(T):
                    mm = pe.transpose(bank[0:H, t * P:(t + 1) * P], pnat[:, t, :], ident[:])
                mm.then_inc(pnt_ps, 1)

            def project_out(b, t):
                bank = claim(pe, b, "c", t)
                rows = slice(t * P, (t + 1) * P)
                if t == 0:
                    pe.wait_ge(o_drained, at(b, PAIRS, PAIRS - 1))
                    drained(pe, b, "pnt", 0)
                pe.matmul(bank[:], pnt[:, rows], nvw[:], start=True, stop=False)
                for q in range(PAIRS):
                    if t == 0 and q == PAIRS - 1:
                        pe.wait_ge(o_drained, at(b, PAIRS, PAIRS))
                    for o, w in ((ot_hi, wo_hi), (ot_hi, wo_lo), (ot_lo, wo_hi)):
                        mm = pe.matmul(bank[:], o[:, q, rows], w[:, q, :], start=False, stop=q == PAIRS - 1 and o is ot_lo)
                mm.then_inc(c_ps, 1)

            def fill(name, i, b):
                if name == "xt":
                    turn_x(b, i)
                elif name == "kv":
                    keys_values(b, "kv", kv_ps, H)
                elif name == "nul":
                    keys_values(b, "nul", nul_ps, 0)
                elif name == "kvn":
                    turn_kv(b)
                elif name == "nn":
                    turn_null(b)
                elif name in ("q0", "q1"):
                    project_q(b, int(name[1]), i)
                elif name == "pnt":
                    turn_null_probs(b)
                else:
                    project_out(b, i)

            def run(b, p):
                fb, fp = pair(b, p + 1)
                for what, i in ORDER:
                    if what == "qt" and pair(b, p + 2)[0] is not None:
                        if pair(b, p + 2)[1] == 0:
                            turn_k(pair(b, p + 2)[0])
                        turn_q(*pair(b, p + 2))
                    elif what == "qk" and fb is not None:
                        scores(fb, fp, i)
                    elif what == "fill":
                        for f in fillers(b, p, i):
                            fill(*f)
                    elif what == "pt" and exists(b):
                        turn_probs(b, p, i)
                    elif what == "pv" and exists(b):
                        weigh_values(b, p, i)

            iterations(pe, run)

        @block.scalar
        def _(act):
            def hi_weights(k):
                act.wait_ge(stage_in[k % 2], 16 * (k // 2 + 1))
                if k < KC:
                    act.activation(wq_hi[:, k, :], stage[k % 2], ACT.Copy, scale=g_col[:, k:k + 1]).then_inc(hi_made, 1)
                elif k == KC:
                    act.wait_ge(wn_made, KC)
                    for j in range(KC):
                        act.activation(wkv_hi[:, j, H:], stage[0][:, j * P:(j + 1) * P], ACT.Copy, scale=g_col[:, j:j + 1])
                        a = act.activation(wkv_hi[:, j, 0:H], wn[:, j, :], ACT.Copy, scale=g_col[:, j:j + 1])
                    a.then_inc(hi_made, 1)
                else:
                    j = k - KC - 1
                    act.activation(wo_hi[:, 2 * j:2 * j + 2, :].rearrange("p a n -> p (a n)"), stage[k % 2], ACT.Copy
                                   ).then_inc(hi_made, 1)

            act.wait_ge(rows_in, ROWS_IN)
            for layer in range(2):
                act.wait_ge(z_gain, layer + 1)
                act.activation(ez, z, ACT.Exp, scale=-1.0).then_inc(z_exp, 1)
                for m in range(T):
                    act.wait_ge(h_turned, T * layer + m + 1)
                    act.activation(ht[:, :, m * P:(m + 1) * P],
                                   [ps_s[0], ps_s[1], ps_pt[0], ps_pt[1]][m][:, :].rearrange("p (k n) -> p k n", k=KC),
                                   ACT.Copy).then_inc(h_drained, 1)
                if layer == 0:
                    for k in range(KC):
                        hi_weights(k)
            for k in range(KC, 2 * KC + 1):
                hi_weights(k)
            act.wait_ge(nvw_acc, PAIRS // 2)
            act.wait_ge(zeros, 2)
            act.activation(nvw[0:H, :], ps_g[0][0:H, :], ACT.Copy)
            act.activation(nvw[2 * Q:2 * Q + H, :], ps_g[0][0:H, :], ACT.Copy).then_inc(nvw_hi_made, 1)

            def fill_stage(name, i, b, s):
                if name == "xt":
                    bank, _ = bank_of(b, name, i)
                    act.wait_ge(xt_ps, at(b, T, i + 1))
                    act.activation(xt_hi[:, :, i * P:(i + 1) * P], bank[:, :].rearrange("p (k n) -> p k n", k=KC),
                                   ACT.Copy).then_inc(xt_hi_made, 1)
                elif name == "kv":
                    bank, done = bank_of(b, name, i)
                    act.wait_ge(kv_ps, at(b, 1, 1))
                    act.activation(kvt, bank[:], ACT.Copy).then_inc(done, 1)
                elif name == "nul":
                    bank, done = bank_of(b, name, i)
                    act.wait_ge(nul_ps, at(b, 1, 1))
                    act.wait_ge(tab_out, 16 * H)
                    act.activation(nt[:, 0:N], bank[0:H, :], ACT.Copy).then_inc(done, 1)
                elif name == "kvn":
                    bank, _ = bank_of(b, name, i)
                    act.wait_ge(kvn_ps, at(b, 1, 1))
                    act.wait_ge(qss_made, at(b, 2 * T, 1))
                    act.activation(ksq, bank[:, :].rearrange("p (t n) -> p t n", t=T)[:, :, 0:DH],
                                   ACT.Square).then_inc(ksq_made, 1)
                elif name in ("q0", "q1"):
                    n = at(b, 2 * T, T * int(name[1]) + i)
                    bank, _ = bank_of(b, name, i)
                    wait(act, qss_made, n)
                    if name == "q0" and i == 1:
                        act.wait_ge(kss_made, at(b, 1, 1))
                    act.wait_ge(q_ps, n + 1)
                    act.activation(qsq[:], bank[:, :].rearrange("p (h d) -> p h d", h=HC), ACT.Square).then_inc(qsq_made, 1)
                elif name == "pnt":
                    bank, _ = bank_of(b, name, i)
                    act.wait_ge(pnt_ps, at(b, 1, 1))
                    act.activation(pnt[0:H, :], bank[0:H, :], ACT.Copy)
                    act.activation(pnt[Q:Q + H, :], bank[0:H, :], ACT.Copy).then_inc(pnh_made, 1)

            def run(b, p):
                fb, fp = pair(b, p + 1)
                for step, (what, i) in enumerate(ORDER):
                    if what == "qt" and pair(b, p + 2)[0] is not None:
                        qb_, qp = pair(b, p + 2)
                        act.wait_ge(qa_ready, at(qb_, PAIRS, qp + 1))
                        act.activation(qb[qp % 2][0:DH], ps_qt[0:DH], ACT.Copy).then_inc(qb_ready, 1)
                    elif what == "qk" and fb is not None:
                        h, t = TILE_OF[i]
                        s = slot(fp, h)
                        act.wait_ge(biased, at(fb, 64, 8 * fp + i + 1))
                        if i % T == 0:
                            wait(act, den_ready, at(fb, H, 2 * fp + h - HEADSLOTS + 1))
                        e = pr[:, s, S_AT[t]:S_AT[t] + S_N[t]]
                        act.activation(e, e, ACT.Exp, bias=mn[:, s, t:t + 1], scale=-1.0,
                                       accum_out=rs[:, s, t:t + 1]).then_inc(exp_done, 1)
                    elif what == "pt" and exists(b) and i not in PT_BY_DVE:
                        drain_group(act, b, p, i)
                    elif what == "pv" and i == 2 and exists(b):
                        act.wait_ge(pv_done, at(b, 3 * PAIRS, 3 * p + 3))
                        if p == 0:
                            wait(act, c_ps, at(b, T, 0))
                        act.activation(ot_hi[:, p, :], ps_o[:], ACT.Copy).then_inc(oh_made, 1)
                    for f in stages(ACT_STAGES, b, p, step):
                        fill_stage(*f)
                    if step in PN_AT and fb is not None:
                        h = PN_AT.index(step)
                        s = slot(fp, h)
                        act.wait_ge(dn_ready, at(fb, H, 2 * fp + h + 1))
                        act.activation(pn[:, s, :], dn[:, s, :], ACT.Exp, scale=-1.0).then_inc(pn_ready, 1)

            def drain_group(act, b, p, g):
                n = GROUPS * p + g
                act.wait_ge(pt_ps, at(b, GROUPS * PAIRS, n + 1))
                wait(act, pv_done, at(b, 3 * PAIRS, slot_free(n)))
                act.activation(pts[:, n % PSLOTS, :], ps_pt[n % 2][:], ACT.Copy).then_inc(pt_drained[n % 2], 1)

            iterations(act, run)

        @block.gpsimd
        def _(pool):
            pool.memset(ident[:], 0.0).then_inc(id_zero, 1)
            pool.memset(half[:], -0.5).then_inc(consts, 1)
            pool.memset(eps[:], EPS).then_inc(consts, 1)
            pool.memset(nv_blk, 0.0).then_inc(consts, 1)
            pool.iota(dist[:], pattern=[[-P, T]], base=N - 1, channel_multiplier=-1,
                      allow_small_or_imprecise_dtypes=True).then_inc(consts, 1)
            pool.wait_ge(id_zero, 1)
            pool.affine_select(out=ident[:], in_=ident[:], compare_op=ALU.not_equal, fill=1.0, base=0,
                               pattern=[[-1, P]], channel_multiplier=1).then_inc(id_made, 1)
            pool.wait_ge(consts, 4)

            def root(dst, src, width, ready):
                pool.tensor_tensor(dst, src, half[:, 0:width], ALU.pow).then_inc(ready, 1)

            pool.wait_ge(vec, 3)
            root(nk_ss[:, 2:3], nk_ss[:, 1:2], 1, nk_pow)
            for layer in range(2):
                pool.wait_ge(z_mv, layer + 1)
                pool.tensor_tensor(ve[:], mv[:, :, 1], eps[:], ALU.add).then_inc(z_ve, 1)
                pool.wait_ge(z_ve, layer + 1)
                root(rstd[:], ve[:], T, z_rstd)

            def fill_stage(name, i, b, s):
                if name == "xt":
                    pool.wait_ge(mv_ready, at(b, T, i + 1))
                    pool.tensor_tensor(ve[:, i:i + 1], mv[:, i, 1:2], eps[:, 0:1], ALU.add).then_inc(ve_made, 1)
                    pool.wait_ge(ve_made, at(b, T, i + 1))
                    root(rstd[:, i:i + 1], ve[:, i:i + 1], 1, rstd_ready)
                elif name == "kvn":
                    pool.wait_ge(kssg_made, at(b, 1, 1))
                    root(rk[:], kssg[:], T, rk_ready)
                elif name in ("q0", "q1"):
                    c = int(name[1])
                    n = at(b, 2 * T, T * c + i)
                    if s == 0:
                        pool.wait_ge(qssg_made, n + 1)
                        root(rq[:, i % 2, :], qssg[:, i % 2, :], HC, rq_ready)
                        return
                    if c == 0 and i == 0:
                        drained(pool, b, "nn", 0)
                    pool.wait_ge(rq_ready, n + 1)
                    pool.tensor_tensor(nsq[:], nsr[:, i, c * HC:(c + 1) * HC], rq[:, i % 2, :], ALU.mult).then_inc(nsq_made, 1)
                    pool.wait_ge(nsq_made, n + 1)
                    pool.tensor_tensor(nsn[:, i, c * HC:(c + 1) * HC], nsq[:], nb_row[:, c * HC:(c + 1) * HC],
                                       ALU.subtract).then_inc(nsn_ready, 1)
                elif name == "c":
                    pool.wait_ge(cmv_ready, at(b, T, i + 1))
                    pool.tensor_tensor(cve[:, i % 2, :], cmv[:, i % 2, 1:2], eps[:, 0:1], ALU.add).then_inc(cve_made, 1)
                    pool.wait_ge(cve_made, at(b, T, i + 1))
                    root(crs[:, i % 2, :], cve[:, i % 2, :], 1, crs_ready)

            def null_score(b, p, h):
                s = slot(p, h)
                pool.wait_ge(biased, at(b, 64, 8 * p + T * (h + 1)))
                pool.tensor_tensor(dn[:, s, :], nsn[:, :, 2 * p + h], mn[:, s, :], ALU.subtract).then_inc(dn_ready, 1)

            def denominator(b, p, h):
                s = slot(p, h)
                pool.wait_ge(pn_ready, at(b, H, 2 * p + h + 1))
                pool.tensor_tensor(den[:, s, :], rs[:, s, :], pn[:, s, :], ALU.add).then_inc(den_ready, 1)

            def normalise(b, p, h):
                s = slot(p, h)
                pool.wait_ge(rr_ready, at(b, H, 2 * p + h + 1))
                if p == 0 and h == 0:
                    wait(pool, pnt_ps, at(b, 1, 0))
                pool.tensor_tensor(pnat[:, :, 2 * p + h], pn[:, s, :], rr[:, s, :], ALU.mult).then_inc(pnat_ready, 1)
                for t in range(T):
                    e = pr[:, s, S_AT[t]:S_AT[t] + S_N[t]]
                    m = pool.tensor_tensor(e, e, rr[:, s, t:t + 1].broadcast_to([P, S_N[t]]), ALU.mult)
                m.then_inc(normed, 1)

            def run(b, p):
                fb, fp = pair(b, p + 1)
                for step in range(STEPS):
                    if fb is not None:
                        if step in DN_AT:
                            null_score(fb, fp, DN_AT.index(step))
                        if step in DEN_AT:
                            denominator(fb, fp, DEN_AT.index(step))
                        if step in RR_AT:
                            normalise(fb, fp, RR_AT.index(step))
                    for f in stages(POOL_STAGES, b, p, step):
                        fill_stage(*f)

            iterations(pool, run)

        @block.vector
        def _(dve):
            dve.wait_ge(id_made, 1)
            dve.tensor_copy(ident16[:], ident[:]).then_inc(id_made, 1)
            for i in range(2):
                dve.memset(qb[i][DH:DH + 1], PADK)
            dve.memset(nvw[:].bitcast(F32), 0.0).then_inc(zeros, 1)
            dve.memset(pnt[:].bitcast(F32), 0.0).then_inc(zeros, 1)
            dve.wait_ge(rows_in, ROWS_IN)
            dve.wait_ge(consts, 4)
            dve.scalar_tensor_tensor(s_row[:], s_row[:], -SCALE, ks_row[:], ALU.mult, ALU.mult).then_inc(vec, 1)
            dve.tensor_tensor_reduce(nk_sq, nk_row[:], nk_row[:], 1.0, 0.0, ALU.mult, ALU.add, nk_ss[:, 0:1]).then_inc(vec, 1)
            dve.wait_ge(vec, 2)
            dve.tensor_scalar(nk_ss[:, 1:2], nk_ss[:, 0:1], 1e-24, None, ALU.max).then_inc(vec, 1)
            dve.wait_ge(nk_pow, 1)
            dve.scalar_tensor_tensor(nk_row[:], nk_row[:], nk_ss[:, 2:3], s_row[:], ALU.mult, ALU.mult).then_inc(vec, 1)
            for h in range(2):
                dst = nv_blk[h * DH:(h + 1) * DH, :, :].rearrange("p a b -> p (a b)")[:, h:h + (H + 2) * (PAIRS - 1) + 1:H + 2]
                dve.tensor_copy(dst, nv_col[h * DH:(h + 1) * DH, :].broadcast_to([DH, PAIRS])).then_inc(vec, 1)
            dve.memset(tab[:, N:RW], MASKED).then_inc(tab_made, 1)
            dve.memset(kb[:], 0.0).then_inc(vec, 1)
            dve.wait_ge(vec, 7)

            def lo_weights(k):
                f = stage[k % 2]
                dve.wait_ge(hi_made, k + 1)
                if k < KC:
                    dve.scalar_tensor_tensor(wq_lo[:, k, :], f, g_col[:, k:k + 1], wq_hi[:, k, :].bitcast(F32),
                                             ALU.mult, ALU.subtract)
                    if k:
                        dve.wait_ge(wn_made, k)
                    dve.tensor_tensor(prod.rearrange("p (h d) -> p h d", h=H), f.rearrange("p (h d) -> p h d", h=H),
                                      nk_row[:].unsqueeze(1).broadcast_to([P, H, DH]), ALU.mult).then_inc(stage_read, 1)
                    dve.wait_ge(stage_read, k + 1)
                    dve.tensor_reduce(wn[:, k, :], prod.rearrange("p (h d) -> p h d", h=H), AX.X, ALU.add).then_inc(wn_made, 1)
                elif k == KC:
                    for j in range(KC):
                        dve.scalar_tensor_tensor(wkv_lo[:, j, 0:H], wn[:, j, :], g_col[:, j:j + 1],
                                                 wkv_hi[:, j, 0:H].bitcast(F32), ALU.mult, ALU.subtract)
                        a = dve.scalar_tensor_tensor(wkv_lo[:, j, H:], f[:, j * P:(j + 1) * P], g_col[:, j:j + 1],
                                                     wkv_hi[:, j, H:].bitcast(F32), ALU.mult, ALU.subtract)
                    a.then_inc(stage_read, 1)
                else:
                    j = k - KC - 1
                    dst = wo_lo[:, 2 * j:2 * j + 2, :].rearrange("p a n -> p (a n)")
                    hi = wo_hi[:, 2 * j:2 * j + 2, :].rearrange("p a n -> p (a n)").bitcast(F32)
                    dve.tensor_tensor(dst, f, hi, ALU.subtract).then_inc(stage_read, 1)

            for layer in range(2):
                for m in range(T):
                    if layer == 0:
                        dve.scalar_tensor_tensor(z[:, m, :], row_w0, dist[:, m:m + 1], row_b0, ALU.mult, ALU.add).then_inc(z_sum, 1)
                    else:
                        dve.wait_ge(h_mm, m + 1)
                        bank = [ps_s[0], ps_s[1], ps_pt[0], ps_pt[1]][m]
                        dve.tensor_tensor(z[:, m, :], bank[:], row_b1, ALU.add).then_inc(z_sum, 1)
                for m in range(T):
                    dve.wait_ge(z_sum, T * layer + m + 1)
                    dve.bn_stats(bn6[:, m, :], z[:, m, :]).then_inc(z_stats, 1)
                dve.wait_ge(z_stats, T * (layer + 1))
                for m in range(T):
                    a = dve.bn_aggr(mv[:, m, :], bn6[:, m, :])
                a.then_inc(z_mv, 1)
                dve.wait_ge(z_rstd, layer + 1)
                for m in range(T):
                    dve.tensor_scalar(z[:, m, :], z[:, m, :], mv[:, m, 0:1], rstd[:, m:m + 1], ALU.subtract, ALU.mult
                                      ).then_inc(z_norm, 1)
                dve.wait_ge(z_norm, T * (layer + 1))
                gain = (row_g0, row_g1)[layer].unsqueeze(1).broadcast_to([P, T, D])
                dve.tensor_tensor(z, z, gain, ALU.mult).then_inc(z_gain, 1)
                dve.wait_ge(z_exp, layer + 1)
                dve.tensor_scalar(ez, ez, 1.0, None, ALU.add).then_inc(z_step, 1)
                dve.wait_ge(z_step, 2 * layer + 1)
                dve.reciprocal(ez, ez).then_inc(z_step, 1)
                dve.wait_ge(z_step, 2 * layer + 2)
                dve.tensor_tensor(z, z, ez, ALU.mult).then_inc(z_act, 1)
                if layer == 0:
                    for k in range(KC):
                        lo_weights(k)
            dve.wait_ge(tab_ps, 1)
            dve.tensor_scalar(tab[:, 0:N], ps_o[0:H, :], b2_col[:], -1.0, ALU.add, ALU.mult).then_inc(tab_made, 1)
            for k in range(KC, 2 * KC + 1):
                lo_weights(k)
            dve.wait_ge(nvw_hi_made, 1)
            dve.tensor_tensor(nvw[Q:Q + H, :], ps_g[0][0:H, :], nvw[0:H, :].bitcast(F32), ALU.subtract).then_inc(weights, 1)

            def rows_of_x(b, t, s):
                bank, done = bank_of(b, "xt", t)
                if s == 0:
                    dve.wait_ge(x_in[t % 2], at(b, 32, 16 * (t // 2 + 1)))
                    dve.bn_stats(bn6[:, t, :], xs[:, t % 2, :]).then_inc(stats, 1)
                    wait_apart(stats, at(b, T, t + 1))
                    dve.bn_aggr(mv[:, t, :], bn6[:, t, :]).then_inc(mv_ready, 1)
                elif s == 1:
                    dve.wait_ge(rstd_ready, at(b, T, t + 1))
                    dve.tensor_scalar(xs[:, t % 2, :], xs[:, t % 2, :], mv[:, t, 0:1], rstd[:, t:t + 1], ALU.subtract, ALU.mult
                                      ).then_inc(xn_ready, 1)
                else:
                    dve.wait_ge(xt_hi_made, at(b, T, t + 1))
                    dst, hi = (a[:, :, t * P:(t + 1) * P] for a in (xt_lo, xt_hi))
                    dve.tensor_tensor(dst, bank[:, :].rearrange("p (k n) -> p k n", k=KC), hi.bitcast(F32),
                                      ALU.subtract).then_inc(done, 1)

            def keys(b, s):
                bank, done = bank_of(b, "kvn", 0)
                rows = bank[:, :].rearrange("p (t n) -> p t n", t=T)
                if s == 0:
                    dve.wait_ge(ksq_made, at(b, 1, 1))
                    dve.tensor_reduce(kss[:], ksq, AX.X, ALU.add).then_inc(kss_made, 1)
                    dve.tensor_copy(vst[:], rows[:, :, DH:]).then_inc(vst_made, 1)
                    dve.wait_ge(kss_made, at(b, 1, 1))
                    dve.tensor_scalar(kssg[:], kss[:], 1e-24, None, ALU.max).then_inc(kssg_made, 1)
                    return
                dve.wait_ge(rk_ready, at(b, 1, 1))
                for t in range(T):
                    a = dve.scalar_tensor_tensor(kh[:, t, :], rows[:, t, 0:DH], rk[:, t:t + 1], s_row[:], ALU.mult, ALU.mult)
                a.then_inc(done, 1)
                drained(dve, b, "kvn", 0)
                wait(dve, kt_ps, at(b, 1, 0))
                hi = knat[:, :, 0:2 * DH].rearrange("p t (a d) -> p t a d", a=2)
                dve.tensor_copy(hi, kh.unsqueeze(2).broadcast_to([P, T, 2, DH])).then_inc(khi_made, 1)
                dve.wait_ge(khi_made, at(b, 1, 1))
                dve.tensor_tensor(knat[:, :, 2 * DH:], kh, knat[:, :, 0:DH], ALU.subtract).then_inc(kn_ready, 1)

            def settle_kv(b):
                bank, done = bank_of(b, "kt", 0)
                f16 = bank[:, :].bitcast(F16)
                dve.wait_ge(kt_ps, at(b, 1, 1))
                dve.tensor_copy(ka[:], f16[:, 0:N])
                dve.tensor_copy(kb[0:DH, :], f16[0:DH, N:]).then_inc(done, 1)
                dve.wait_ge(mask_in, at(b, 16, 16))
                dve.tensor_scalar(kb[DH:DH + 1, :], mask_u8[DH:DH + 1, :], -PADK, PADK, ALU.mult, ALU.add).then_inc(kv_ready, 1)

            def settle_v(b):
                wait(dve, pv_done, at(b, 3 * PAIRS, 0))
                dve.wait_ge(vst_made, at(b, 1, 1))
                dve.tensor_copy(v[:], vst[:]).then_inc(v_ready, 1)

            def split_q(b, c, i, s):
                n = at(b, 2 * T, T * c + i)
                bank, done = bank_of(b, f"q{c}", i)
                if s == 0:
                    dve.wait_ge(qsq_made, n + 1)
                    dve.tensor_reduce(qss[:], qsq[:], AX.X, ALU.add).then_inc(qss_made, 1)
                    dve.wait_ge(qss_made, n + 1)
                    wait(dve, rq_ready, n - 1)
                    dve.tensor_scalar(qssg[:, i % 2, :], qss[:], 1e-24, None, ALU.max).then_inc(qssg_made, 1)
                    return
                if c == 0 and i == 1:
                    dve.wait_ge(kn_ready, at(b, 1, 1))
                else:
                    wait(dve, qn_ready, n)
                dve.wait_ge(rq_ready, n + 1)
                dve.tensor_tensor(qf[:], bank[:, :].rearrange("p (h d) -> p h d", h=HC),
                                  rq[:, i % 2, :].unsqueeze(2).broadcast_to([P, HC, DH]), ALU.mult).then_inc(done, 1)
                drained(dve, b, f"q{c}", i)
                dve.tensor_copy(qn[c][:, i, :, 0:DH], qf[:]).then_inc(qhi_made, 1)
                dve.wait_ge(qhi_made, n + 1)
                dve.tensor_tensor(qn[c][:, i, :, DH:], qf[:], qn[c][:, i, :, 0:DH], ALU.subtract).then_inc(qn_ready, 1)

            def finish_rows(b, t, s):
                bank, done = bank_of(b, "c", t)
                if s == 0:
                    dve.wait_ge(c_ps, at(b, T, t + 1))
                    dve.bn_stats(cbn6[:], bank[:]).then_inc(cstats, 1)
                    wait_apart(cstats, at(b, T, t + 1))
                    dve.bn_aggr(cmv[:, t % 2, :], cbn6[:]).then_inc(cmv_ready, 1)
                    dve.wait_ge(cmv_ready, at(b, T, t + 1))
                    dve.scalar_tensor_tensor(bank[:], bank[:], cmv[:, t % 2, 0:1], gout_row[:], ALU.subtract, ALU.mult
                                             ).then_inc(og_made, 1)
                    return
                dve.wait_ge(og_made, at(b, T, t + 1))
                dve.wait_ge(crs_ready, at(b, T, t + 1))
                dve.wait_ge(res_in[t % 2], at(b, 16 * (T // 2), 16 * (t // 2 + 1)))
                dve.scalar_tensor_tensor(res[t % 2][:], bank[:], crs[:, t % 2, :], res[t % 2][:], ALU.mult, ALU.add).then_inc(done, 1)

            def fill_stage(name, i, b, s):
                bank, done = bank_of(b, name, i)
                if name == "xt":
                    rows_of_x(b, i, s)
                elif name == "kvn":
                    keys(b, s)
                elif name == "nn":
                    dve.wait_ge(nn_ps, at(b, 1, 1))
                    wait(dve, nsn_ready, at(b, 2 * T, 0))
                    dve.tensor_copy(nsr[:], bank[:, 0:T * H].rearrange("p (t h) -> p t h", t=T)).then_inc(done, 1)
                elif name in ("q0", "q1"):
                    split_q(b, int(name[1]), i, s)
                elif name == "pnt":
                    dve.wait_ge(pnh_made, at(b, 1, 1))
                    dve.tensor_tensor(pnt[2 * Q:2 * Q + H, :], bank[0:H, :], pnt[0:H, :].bitcast(F32), ALU.subtract).then_inc(done, 1)
                elif name == "c":
                    finish_rows(b, i, s)

            def add_bias(b, p, i):
                h, t = TILE_OF[i]
                s = slot(p, h)
                if i == 0:
                    dve.wait_ge(tb_in[p % 2], at(b, 16 * PAIRS // 2, 16 * (p // 2 + 1)))
                    dve.wait_ge(nsn_ready, at(b, 2 * T, T * (p // (HC // 2)) + T))
                    wait(dve, pt_ps, at(b, GROUPS * PAIRS, GROUPS * (p - 1)))
                    wait(dve, dn_ready, at(b, H, 2 * p - 2))
                wait_apart(qk_ps, at(b, 64, 8 * p + i + 1))
                off = (T - 1 - t) * P
                dve.tensor_tensor_reduce(pr[:, s, S_AT[t]:S_AT[t] + S_N[t]], ps_s[i % 2][:, 0:S_N[t]],
                                         tb[p % 2][:, h, off:off + S_N[t]], 1.0, nsn[:, t, 2 * p + h:2 * p + h + 1],
                                         ALU.add, ALU.min, mn[:, s, t:t + 1]).then_inc(biased, 1)

            def invert(b, p, h):
                s = slot(p, h)
                dve.wait_ge(den_ready, at(b, H, 2 * p + h + 1))
                dve.reciprocal(rr[:, s, :], den[:, s, :]).then_inc(rr_ready, 1)

            def run(b, p):
                fb, fp = pair(b, p + 1)
                for step, (what, i) in enumerate(ORDER):
                    if what == "qt" and pair(b, p + 2)[0] is not None:
                        qb_, qp = pair(b, p + 2)
                        if qp == 0:
                            settle_kv(qb_)
                        dve.wait_ge(qt_ps, at(qb_, PAIRS, qp + 1))
                        dve.tensor_copy(qa[qp % 2][:], ps_qt[:]).then_inc(qa_ready, 1)
                    elif what == "qk" and fb is not None:
                        add_bias(fb, fp, i)
                    elif what == "pt" and exists(b) and i in PT_BY_DVE:
                        n = GROUPS * p + i
                        dve.wait_ge(pt_ps, at(b, GROUPS * PAIRS, n + 1))
                        wait(dve, pv_done, at(b, 3 * PAIRS, slot_free(n)))
                        dve.tensor_copy(pts[:, n % PSLOTS, :], ps_pt[n % 2][:]).then_inc(pt_drained[n % 2], 1)
                    elif what == "pv" and i == 2 and exists(b):
                        dve.wait_ge(oh_made, at(b, PAIRS, p + 1))
                        dve.tensor_tensor(ot_lo[:, p, :], ps_o[:], ot_hi[:, p, :].bitcast(F32), ALU.subtract).then_inc(o_drained, 1)
                    for f in stages(DVE_STAGES, b, p, step):
                        fill_stage(*f)
                    if step in RR_AT and fb is not None:
                        invert(fb, fp, RR_AT.index(step))
                if p == PAIRS - 1 and fb is not None:
                    settle_v(fb)

            iterations(dve, run)


ROWS_IN = 16 * 15
_INS = ["x", "cond_64", "mask_BxS_bf1", "L0_cond_g_norm", "L0_cond_Wq", "L0_cond_Wkv", "L0_cond_q_scale",
        "L0_cond_k_scale", "L0_cond_null_attn_bias", "L0_cond_w0", "L0_cond_b0", "L0_cond_g0", "L0_cond_w1",
        "L0_cond_b1", "L0_cond_g1", "L0_cond_w2", "L0_cond_b2", "L0_cond_Wout", "L0_cond_g_out"]


def kernel(**inputs):
    import numpy as _np
    import concourse.bacc as _bacc
    from concourse import mybir as _mybir
    from concourse.bass_utils import run_bass_kernel_spmd as _run

    nc = _bacc.Bacc("TRN2", target_bir_lowering=False, num_devices=1)
    arrays, args = {}, []
    for name in _INS:
        a = _np.ascontiguousarray(inputs[name])
        if a.dtype == _np.bool_:
            a = a.view(_np.uint8)
        arrays[name] = a
        args.append(nc.dram_tensor(name, a.shape, _mybir.dt.from_np(a.dtype), kind="ExternalInput").ap())
    out = nc.dram_tensor("out", (B, N, D), _mybir.dt.float32, kind="ExternalOutput").ap()
    build(nc, *args, out)
    r = _run(nc, [arrays], core_ids=[0])
    return r.results[0]["out"]
```

```python
import numpy as np
import concourse.bass as bass
from concourse import mybir
from contextlib import ExitStack

B, N, D = 8, 512, 512
H, DH = 16, 64
P = 128
Q = 32
T = N // P
KC = D // P
PAIRS = H // 2
CH = 2
HC = H // CH
SCALE = 8.0
EPS = 1e-5
MASKED = 1e30
PADK = 32768.0
RW = N + P
HEADSLOTS = 4
GROUPS = 5
PSLOTS = 4
S_AT = [P * t * (t + 1) // 2 for t in range(T)]
S_N = [P * (t + 1) for t in range(T)]
S_ALL = sum(S_N)
GROUP = [[(0, 0, 0)], [(0, 1, 0), (0, 3, 384)], [(1, 0, 0)], [(1, 1, 0), (1, 3, 384)], [(0, 2, 0), (1, 2, 256)]]
PV_SETS = [[(0, ((0, 0), (2, 0)))], [(1, ((1, 0), (3, 0))), (3, ((1, 384), (3, 384)))], [(2, ((4, 0), (4, 256)))]]
PV_NEEDS = [2, 3, 4]
PV_FREES = {0: 0, 2: 0, 1: 1, 3: 1, 4: 2}
ORDER = [('qk', 0), ('qk', 1), ('fill', 0), ('qk', 2), ('pt', 0), ('qk', 3), ('pt', 1), ('qk', 4),
         ('fill', 1), ('qk', 5), ('pt', 2), ('qk', 6), ('pt', 3), ('qk', 7), ('qt', 0), ('fill', 2),
         ('pt', 4), ('pv', 0), ('pv', 1), ('pv', 2)]
STEPS = len(ORDER)
TILE_OF = [(0, 3), (0, 2), (0, 1), (0, 0), (1, 3), (1, 2), (1, 1), (1, 0)]
FILL = {
    0: [[('c', 0, -1)], [('c', 1, -1)], [('c', 2, -1), ('c', 3, -1)]],
    1: [[('q1', 1, 0)], [('q1', 2, 0)], []],
    2: [[('q1', 3, 0)], [], [('xt', 0, 1)]],
    3: [[('xt', 1, 1)], [], [('xt', 2, 1), ('xt', 3, 1)]],
    4: [[('nul', 0, 1), ('kv', 0, 1), ('nn', 0, 1)], [('q0', 0, 1)], [('kvn', 0, 1)]],
    5: [[('q0', 1, 1)], [('q0', 2, 1)], []],
    6: [[('q0', 3, 1)], [], []],
    7: [[], [('pnt', 0, 0)], [('q1', 0, 1)]],
}
DVE_STAGES = {
    'kvn': [1, 6], 'nn': [3], 'pnt': [3], ('q0', 0): [-1, 8, 10], ('q0', 1): [1, 5, 11],
    ('q0', 2): [-1, 5, 7], ('q0', 3): [-1, 5, 7], ('q1', 0): [-2, 6, 9], ('q1', 1): [1, 5, 9],
    ('q1', 2): [1, 6, 8], ('q1', 3): [1, 5, 7], ('xt', 0): [-12, -6, 3], ('xt', 1): [-8, -5, 4],
    ('xt', 2): [-12, -7, 2], ('xt', 3): [-12, -6, 2], ('c', 0): [1, 2], ('c', 1): [1, 2], ('c', 2): [0, 3],
    ('c', 3): [3, 4],
}
ACT_STAGES = {
    'kv': [-1], 'nul': [-1], 'kvn': [0], 'pnt': [0], ('xt', 0): [3], ('xt', 1): [2], ('xt', 2): [-2],
    ('xt', 3): [2], ('q0', 0): [0, 9], ('q0', 1): [-2, 6], ('q0', 2): [-2, 6], ('q0', 3): [0, 5],
    ('q1', 0): [-2, 8], ('q1', 1): [-2, 2], ('q1', 2): [-3, 6], ('q1', 3): [-2, 4],
}
POOL_STAGES = {
    'kvn': [0], ('xt', 0): [-7], ('xt', 1): [-8], ('xt', 2): [-15], ('xt', 3): [-7], ('c', 0): [1],
    ('c', 1): [1], ('c', 2): [-2], ('c', 3): [1], ('q0', 0): [1, 6], ('q0', 1): [1, 6], ('q0', 2): [1, 6],
    ('q0', 3): [1, 7], ('q1', 0): [0, 3], ('q1', 1): [2, 3], ('q1', 2): [0, 5], ('q1', 3): [0, 4],
}
DN_AT, PN_AT, DEN_AT, RR_AT, NORM_AT = [5, 10], [5, 17], [5, 15], [9, 18], [9, 19]
QA_AT, QB_AT = 13, 14
PTS_AT = [3, 6, 10, 10, 14]
OH_AT, OL_AT = 19, 19
PT_BY_DVE = (1, 2)


def exists(b):
    return not isinstance(b, int) or 0 <= b < B


def is_first(b):
    return isinstance(b, int) and b == 0


def is_lead_in(b):
    return isinstance(b, int) and b == -1


def pair(b, p):
    if p >= PAIRS:
        b, p = b + 1, p - PAIRS
    return (b, p) if exists(b) else (None, None)


def fillers(b, p, k):
    if p < 0:
        b, p = b - 1, p + PAIRS
    if p >= PAIRS:
        b, p = b + 1, p - PAIRS
    for name, i, offset in FILL[p][k]:
        if exists(b + offset):
            yield name, i, b + offset


def stages(lags, b, p, step):
    for d in (-1, 0, 1):
        for k in range(3):
            for name, i, batch in fillers(b, p + d, k):
                for s, lag in enumerate(lags.get((name, i), lags.get(name, ()))):
                    if ORDER.index(("fill", k)) + lag + d * STEPS == step:
                        yield name, i, batch, s


def iterations(eng, run):
    def batch(b):
        for p in range(1, PAIRS):
            run(b, p)

    for p in range(1, PAIRS):
        run(-1, p)
    run(0, 0)
    batch(0)
    run(1, 0)
    with eng.Fori(1, B - 1) as b:
        batch(b)
        run(b + 1, 0)
    batch(B - 1)
    run(B, 0)


def at(b, per, n):
    return b * per + n


def wait(eng, sem, value):
    if isinstance(value, int) and value <= 0:
        return
    eng.wait_ge(sem, value)


def general_uses():
    uses = {}
    for b in range(-1, B + 1):
        for p in range(PAIRS):
            for what, k in ORDER:
                if what == "fill":
                    for name, i, batch in fillers(b, p, k):
                        uses[batch, name, i] = len(uses)
                elif what == "qt" and pair(b, p + 2)[1] == 0:
                    uses[pair(b, p + 2)[0], "kt", 0] = len(uses)
    return uses


G_USES = general_uses()
G_PER = G_USES[3, "c", 0] - G_USES[2, "c", 0]


def g_use(b, name, i):
    if isinstance(b, int):
        k = G_USES[b, name, i]
        return k % 2, k // 2
    k = G_USES[2, name, i] - 2 * G_PER
    return k % 2, b * (G_PER // 2) + k // 2


def build(nc, x, cond, mask, g_norm, Wq, Wkv, q_scale, k_scale, null_bias,
          w0, b0, g0, w1, b1, g1, w2, b2, Wout, g_out, out):
    F32, F32R, F16, U8 = mybir.dt.float32, mybir.dt.float32r, mybir.dt.float16, mybir.dt.uint8
    ALU, ACT, AX = mybir.AluOpType, mybir.ActivationFunctionType, mybir.AxisListType

    table = nc.dram_tensor("bias_table", (H, P * RW), F32).ap()

    ctx = ExitStack()
    with ctx:
        def sb(name, shape, dt=F32):
            return ctx.enter_context(nc.sbuf_tensor(name, shape, dt))

        def pb(name, shape, dt=F32):
            return ctx.enter_context(nc.psum_tensor(name, shape, dt))

        def sem(name):
            return ctx.enter_context(nc.semaphore(name))

        wq_hi = sb("wq_hi", [P, KC, H * DH], F32R)
        wq_lo = sb("wq_lo", [P, KC, H * DH], F32R)
        wkv_hi = sb("wkv_hi", [P, KC, H + 2 * DH], F32R)
        wkv_lo = sb("wkv_lo", [P, KC, H + 2 * DH], F32R)
        wo_hi = sb("wo_hi", [P, PAIRS, D], F32R)
        wo_lo = sb("wo_lo", [P, PAIRS, D], F32R)
        nvw = sb("nvw", [3 * Q, D], F32R)
        ident = sb("ident", [P, P])
        ident16 = sb("ident16", [P, P], F16)
        half = sb("half", [P, H])
        eps = sb("eps", [P, T])
        g_col = sb("g_col", [P, KC])
        gout_row = sb("gout_row", [P, D])
        nb_row = sb("nb_row", [P, H])
        s_row = sb("s_row", [P, DH])
        nk_row = sb("nk_row", [P, DH])
        ks_row = sb("ks_row", [P, DH])
        xs = sb("xs", [P, 2, D])
        xt_hi = sb("xt_hi", [P, KC, N], F32R)
        xt_lo = sb("xt_lo", [P, KC, N], F32R)
        bn6 = sb("bn6", [P, T, 6])
        mv = sb("mv", [P, T, 2])
        ve = sb("ve", [P, T])
        rstd = sb("rstd", [P, T])
        kvt = xs[:, 0, :]
        nt = sb("nt", [H, RW])
        kss = sb("kss", [P, T])
        kssg = sb("kssg", [P, T])
        rk = sb("rk", [P, T])
        knat = sb("knat", [P, T, 3 * DH], F16)
        vst = sb("vst", [P, T, DH])
        v = sb("v", [P, T, DH])
        ka = sb("ka", [P, N], F16)
        kb = sb("kb", [P, N], F16)
        mask_u8 = sb("mask_u8", [P, N], U8)
        nsr = sb("nsr", [P, T, H])
        qsq = sb("qsq", [P, HC, DH])
        qss = sb("qss", [P, HC])
        qssg = sb("qssg", [P, 2, HC])
        rq = sb("rq", [P, 2, HC])
        nsq = sb("nsq", [P, HC])
        qf = sb("qf", [P, HC, DH])
        ksq, kh = qsq[:, 0:T, :], qf[:, 0:T, :]
        qn = [sb(f"qn{c}", [P, T, HC, 2 * DH], F16) for c in range(CH)]
        nsn = sb("nsn", [P, T, H])
        qa = [sb(f"qa{i}", [P, 2, N], F16) for i in range(2)]
        qb = [sb(f"qb{i}", [DH + 1, 2, N], F16) for i in range(2)]
        tb = [sb(f"tb{i}", [P, 2, N]) for i in range(2)]
        pr = sb("pr", [P, HEADSLOTS, S_ALL])
        mn = sb("mn", [P, HEADSLOTS, T])
        rs = sb("rs", [P, HEADSLOTS, T])
        dn = sb("dn", [P, HEADSLOTS, T])
        pn = sb("pn", [P, HEADSLOTS, T])
        den = sb("den", [P, HEADSLOTS, T])
        rr = sb("rr", [P, HEADSLOTS, T])
        pnat = sb("pnat", [P, T, H])
        pts = sb("pts", [P, PSLOTS, N])
        ot_hi = sb("ot_hi", [P, PAIRS, N], F32R)
        ot_lo = sb("ot_lo", [P, PAIRS, N], F32R)
        pnt = sb("pnt", [3 * Q, N], F32R)
        cbn6 = sb("cbn6", [P, 6])
        cmv = sb("cmv", [P, 2, 2])
        cve = sb("cve", [P, 2, 1])
        crs = sb("crs", [P, 2, 1])
        res = [sb(f"res{i}", [P, D]) for i in range(2)]

        ps_s = [pb(f"ps_s{i}", [P, N]) for i in range(2)]
        ps_pt = [pb(f"ps_pt{i}", [P, N]) for i in range(2)]
        ps_o = pb("ps_o", [P, N])
        ps_g = [pb(f"ps_g{i}", [P, N]) for i in range(2)]
        ps_qt = pb("ps_qt", [P, 2, N], F16)

        z = pr[:, :, :].rearrange("p a b -> p (a b)")[:, 0:T * D].rearrange("p (t d) -> p t d", t=T)
        ez = pr[:, :, :].rearrange("p a b -> p (a b)")[:, T * D:2 * T * D].rearrange("p (t d) -> p t d", t=T)
        row_w0, row_b0, row_g0, row_b1 = (tb[i // 2][:, i % 2, :] for i in range(4))
        row_g1 = res[0][:, :]
        w1_sb = qn[0][:, :, :, :].rearrange("p a b c -> p (a b c)").bitcast(F32).rearrange("p (k n) -> p k n", k=KC)
        ht = qn[1][:, :, :, :].rearrange("p a b c -> p (a b c)").bitcast(F32).rearrange("p (k n) -> p k n", k=KC)
        stage = [pts[:, 2 * i:2 * i + 2, :].rearrange("p a b -> p (a b)") for i in range(2)]
        prod = pr[:, :, :].rearrange("p a b -> p (a b)")[:, 2 * T * D:2 * T * D + H * DH]
        w2_sb = res[1][:, 0:DH].rearrange("p (k h) -> p k h", k=KC)
        wn = res[1][:, DH:2 * DH].rearrange("p (k h) -> p k h", k=KC)
        nv_blk = res[1][:, 2 * DH:4 * DH].rearrange("p (q h) -> p q h", h=H)
        b2_col = sb("b2_col", [H, 1])
        nv_col = sb("nv_col", [P, 1])
        tab = pr[:, :, :].rearrange("p a b -> p (a b)")[0:H, T * D:T * D + RW]
        dist = sb("dist", [P, T])
        nk_sq = qsq[:, 0, :]
        nk_ss = sb("nk_ss", [P, 3])

        consts = sem("consts"); id_zero = sem("id_zero"); id_made = sem("id_made")
        net_in = sem("net_in"); cols_in = sem("cols_in"); rows_in = sem("rows_in"); w1_in = sem("w1_in"); prod_made = sem("prod_made")
        stage_in = [sem("stage_in0"), sem("stage_in1")]
        hi_made = sem("hi_made"); stage_read = sem("stage_read"); nvw_acc = sem("nvw_acc")
        vec = sem("vec"); nk_pow = sem("nk_pow"); wn_made = sem("wn_made")
        nvw_hi_made = sem("nvw_hi_made"); zeros = sem("zeros"); weights = sem("weights")
        z_sum = sem("z_sum"); z_stats = sem("z_stats"); z_mv = sem("z_mv"); z_ve = sem("z_ve"); z_rstd = sem("z_rstd")
        z_neg = sem("z_neg"); z_exp = sem("z_exp"); z_ln = sem("z_ln"); z_sig = sem("z_sig"); gains = sem("gains"); z_act = sem("z_act")
        h_turned = sem("h_turned"); h_drained = sem("h_drained"); h_mm = sem("h_mm"); tab_ps = sem("tab_ps"); tab_made = sem("tab_made")
        tab_out = sem("tab_out")
        passed = sem("passed")
        x_in = [sem("x_in0"), sem("x_in1")]; stats = sem("stats"); mv_ready = sem("mv_ready"); ve_made = sem("ve_made"); rstd_ready = sem("rstd_ready")
        xn_ready = sem("xn_ready"); xt_ps = sem("xt_ps"); xt_hi_made = sem("xt_hi_made")
        kv_ps = sem("kv_ps"); nul_ps = sem("nul_ps"); kvn_ps = sem("kvn_ps"); nn_ps = sem("nn_ps")
        ksq_made = sem("ksq_made"); kss_made = sem("kss_made"); kssg_made = sem("kssg_made"); rk_ready = sem("rk_ready")
        khi_made = sem("khi_made"); kn_ready = sem("kn_ready"); kt_ps = sem("kt_ps"); mask_in = sem("mask_in")
        kv_ready = sem("kv_ready"); v_ready = sem("v_ready"); vst_made = sem("vst_made")
        q_ps = sem("q_ps"); qsq_made = sem("qsq_made"); qss_made = sem("qss_made"); qssg_made = sem("qssg_made"); rq_ready = sem("rq_ready")
        nsq_made = sem("nsq_made"); nsn_ready = sem("nsn_ready"); qhi_made = sem("qhi_made"); qn_ready = sem("qn_ready")
        g_drained = [sem("g_drained0"), sem("g_drained1")]
        qt_ps = sem("qt_ps"); qa_ready = sem("qa_ready"); qb_ready = sem("qb_ready")
        tb_in = [sem("tb_in0"), sem("tb_in1")]
        qk_ps = sem("qk_ps"); biased = sem("biased"); exp_done = sem("exp_done")
        dn_ready = sem("dn_ready"); pn_ready = sem("pn_ready"); den_ready = sem("den_ready"); rr_ready = sem("rr_ready")
        normed = sem("normed"); pnat_ready = sem("pnat_ready"); pt_ps = sem("pt_ps"); pt_drained = [sem("pt_drained0"), sem("pt_drained1")]
        pv_done = sem("pv_done"); oh_made = sem("oh_made"); o_drained = sem("o_drained")
        pnt_ps = sem("pnt_ps"); pnh_made = sem("pnh_made"); c_ps = sem("c_ps"); cstats = sem("cstats")
        cmv_ready = sem("cmv_ready"); cve_made = sem("cve_made"); crs_ready = sem("crs_ready"); og_made = sem("og_made")
        res_in = [sem("res_in0"), sem("res_in1")]; out_sent = [sem("out_sent0"), sem("out_sent1")]

        def slot(p, h):
            return (2 * p + h) % HEADSLOTS

        def slot_free(n):
            p, g = divmod(n - PSLOTS, GROUPS)
            return 3 * p + PV_FREES[g] + 1

        def wait_apart(sem, value):
            nc.vector.wait_ge(sem, value)
            nc.vector.sem_inc(passed, 1)

        def drained(eng, b, name, i):
            bank, before = g_use(b, name, i)
            eng.wait_ge(g_drained[bank], before + 1)

        def claim(eng, b, name, i):
            bank, before = g_use(b, name, i)
            wait(eng, g_drained[bank], before)
            return ps_g[bank]

        def bank_of(b, name, i):
            return ps_g[g_use(b, name, i)[0]], g_drained[g_use(b, name, i)[0]]

        block = ctx.enter_context(nc.Block())

        @block.sync
        def _(sp):
            def load_x(b, tiles):
                for t in tiles:
                    wait(sp, weights, 0 if is_first(b) else 1)
                    wait(sp, xt_ps, at(b, T, t - 1))
                    if t == 0:
                        wait(sp, kvn_ps, at(b, 1, 0))
                    sp.dma_start(xs[:, t % 2, :], x[bass.ds(b, 1), t * P:(t + 1) * P, :].rearrange("a p d -> (a p) d")
                                 ).then_inc(x_in[t % 2], 16)

            for dst, src in ((row_w0, w0[0, :]), (row_b0, b0), (row_g0, g0)):
                sp.dma_start(dst, src.partition_broadcast(P)).then_inc(net_in, 16)
            for dst, src in ((nk_row[:], cond[0, :]), (s_row[:], q_scale), (ks_row[:], k_scale)):
                sp.dma_start(dst, src.partition_broadcast(P)).then_inc(cols_in, 16)
            sp.dma_start(g_col[:], g_norm.rearrange("(k p) -> p k", p=P),
                         allow_slow_non_contiguous=True).then_inc(cols_in, 16)

            def load_weights(k):
                wait(sp, stage_read, k - 1)
                wait(sp, prod_made, min(k - 1, KC))
                wait(sp, nvw_acc, k - 2 - KC)
                if k < KC:
                    dst, src = stage[k % 2], Wq[k * P:(k + 1) * P, :]
                elif k == KC:
                    dst = stage[0][:, 0:KC * 2 * DH].rearrange("p (k n) -> p k n", k=KC)
                    src = Wkv.rearrange("(k p) n -> p k n", p=P)
                else:
                    j = k - KC - 1
                    dst = stage[k % 2].rearrange("p (a n) -> p a n", a=2)
                    src = Wout[2 * j * P:2 * (j + 1) * P, :].rearrange("(a p) n -> p a n", p=P)
                sp.dma_start(dst, src).then_inc(stage_in[k % 2], 16)

            load_weights(0)
            load_weights(1)
            sp.dma_start(w1_sb, w1.rearrange("(k p) n -> p k n", p=P)).then_inc(w1_in, 16)
            for dst, src in ((row_b1, b1), (row_g1, g1), (nb_row[:], null_bias), (gout_row[:], g_out)):
                sp.dma_start(dst, src.partition_broadcast(P)).then_inc(rows_in, 16)
            sp.dma_start(w2_sb, w2.rearrange("(k p) h -> p k h", p=P)).then_inc(rows_in, 16)
            sp.dma_start(b2_col[:], b2.unsqueeze(1)).then_inc(rows_in, 16)
            for h in range(2):
                sp.dma_start(nv_col[h * DH:(h + 1) * DH, :], cond[1, :].unsqueeze(1)).then_inc(rows_in, 16)
            load_x(0, (0, 1))
            sp.dma_start(mask_u8[DH:DH + 1, :], mask[0:1, :]).then_inc(mask_in, 16)
            for k in range(2, KC + 2):
                load_weights(k)

            def store_table():
                sp.wait_ge(tab_made, 2)
                for h in range(H):
                    sp.dma_start(table[h:h + 1, :].rearrange("a (p u) -> a p u", p=P),
                                 tab[h:h + 1, :].unsqueeze(1).broadcast_to([1, P, RW])).then_inc(tab_out, 16)
                sp.wait_ge(tab_out, 16 * H)

            def load_bias(b, p):
                wait(sp, weights, 0 if is_first(b) else 1)
                wait(sp, biased, at(b, 64, 8 * (p - 1)))
                src = bass.AP(table.tensor, 2 * p * P * RW + P - 1, [[RW - 1, P], [P * RW, 2], [1, N]])
                sp.dma_start(tb[p % 2][:], src).then_inc(tb_in[p % 2], 16)

            def store(b):
                for t in range(2):
                    load_rows(b, t)
                for t in range(T):
                    sp.wait_ge(weights, 1)
                    drained(sp, b, "c", t)
                    sp.dma_start(out[bass.ds(b, 1), t * P:(t + 1) * P, :].rearrange("a p d -> (a p) d"), res[t % 2][:]
                                 ).then_inc(out_sent[t % 2], 16)
                    if t + 2 < T:
                        load_rows(b, t + 2)

            def load_rows(b, t):
                    sp.wait_ge(weights, 1)
                    wait(sp, out_sent[t % 2], at(b, 16 * (T // 2), 16 * (t // 2)))
                    sp.dma_start(res[t % 2][:], x[bass.ds(b, 1), t * P:(t + 1) * P, :].rearrange("a p d -> (a p) d")
                                 ).then_inc(res_in[t % 2], 16)

            def run(b, p):
                nb, np_ = pair(b, p + 2)
                if is_lead_in(b) and p == 5:
                    load_weights(KC + 2)
                    store_table()
                if nb is not None:
                    load_bias(nb, np_)
                if is_lead_in(b) and p in (6, 7):
                    load_weights(KC + p - 3)
                if p == 0 and exists(b - 1):
                    store(b - 1)
                if p == 1 and exists(b + 1) and not is_lead_in(b):
                    load_x(b + 1, (0, 1))
                    sp.wait_ge(weights, 1)
                    sp.wait_ge(kv_ready, at(b, 1, 1))
                    sp.dma_start(mask_u8[DH:DH + 1, :], mask[bass.ds(b + 1, 1), :]).then_inc(mask_in, 16)
                if p == 3 and exists(b + 1):
                    load_x(b + 1, (2, 3))

            iterations(sp, run)
            for i in range(2):
                sp.wait_ge(out_sent[i], 16 * (T // 2) * B)

        @block.tensor
        def _(pe):
            pe.wait_ge(consts, 4)
            pe.wait_ge(id_made, 2)
            banks = [ps_s[0], ps_s[1], ps_pt[0], ps_pt[1]]

            def network(layer):
                for m in range(T):
                    pe.wait_ge(z_act, T * layer + m + 1)
                    for k in range(KC):
                        mm = pe.transpose(banks[m][:, k * P:(k + 1) * P], z[:, m, k * P:(k + 1) * P], ident[:])
                    mm.then_inc(h_turned, 1)
                if layer == 0:
                    pe.wait_ge(w1_in, 16)
                    for m in range(T):
                        pe.wait_ge(h_drained, m + 1)
                        for k in range(KC):
                            mm = pe.matmul(banks[m][:], ht[:, k, m * P:(m + 1) * P], w1_sb[:, k, :],
                                           start=k == 0, stop=k == KC - 1)
                        mm.then_inc(h_mm, 1)
                else:
                    pe.wait_ge(h_drained, 2 * T)
                    pe.wait_ge(rows_in, ROWS_IN)
                    for k in range(KC):
                        mm = pe.matmul(ps_o[0:H, :], w2_sb[:, k, :], ht[:, k, :], start=k == 0, stop=k == KC - 1)
                    mm.then_inc(tab_ps, 1)

            def null_value(j):
                k = KC + 1 + j
                if j == 0:
                    pe.wait_ge(vec, 7)
                    pe.wait_ge(tab_made, 2)
                pe.wait_ge(stage_in[k % 2], 16 * (k // 2 + 1))
                for a in range(2):
                    q = 2 * j + a
                    mm = pe.matmul(ps_o[0:H, :], nv_blk[:, q, :], stage[k % 2][:, a * D:(a + 1) * D],
                                   start=q == 0, stop=q == PAIRS - 1)
                mm.then_inc(nvw_acc, 1)

            network(0)

            def turn_x(b, t):
                bank = claim(pe, b, "xt", t)
                pe.wait_ge(xn_ready, at(b, T, t + 1))
                for k in range(KC):
                    mm = pe.transpose(bank[:, k * P:(k + 1) * P], xs[:, t % 2, k * P:(k + 1) * P], ident[:])
                mm.then_inc(xt_ps, 1)

            def products(bank, pairs):
                for i, (lhs, rhs) in enumerate(pairs):
                    mm = pe.matmul(bank, lhs, rhs, start=i == 0, stop=i == len(pairs) - 1)
                return mm

            def keys_values(b, name, done, col):
                bank = claim(pe, b, name, 0)
                for t in range(T):
                    drained(pe, b, "xt", t)
                cols = slice(col, col + P)
                products(bank[:], [(w[:, k, cols], xt[:, k, :]) for k in range(KC)
                                   for w, xt in ((wkv_hi, xt_hi), (wkv_lo, xt_hi), (wkv_hi, xt_lo))]).then_inc(done, 1)

            def turn_kv(b):
                bank = claim(pe, b, "kvn", 0)
                drained(pe, b, "kv", 0)
                for t in range(T):
                    mm = pe.transpose(bank[:, t * P:(t + 1) * P], kvt[:, t * P:(t + 1) * P], ident[:])
                mm.then_inc(kvn_ps, 1)

            def turn_null(b):
                bank = claim(pe, b, "nn", 0)
                drained(pe, b, "nul", 0)
                pe.transpose(bank[:, P:2 * P], ident[:], ident[:])
                for t in range(T):
                    mm = pe.transpose(bank[:, t * H:(t + 1) * H], nt[:, t * P:(t + 1) * P], ident[0:H, 0:H])
                mm.then_inc(nn_ps, 1)

            def turn_k(b):
                bank = claim(pe, b, "kt", 0)[:, :].bitcast(F16)
                pe.wait_ge(kn_ready, at(b, 1, 1))
                for t in range(T):
                    pe.transpose(bank[:, t * P:(t + 1) * P], knat[:, t, 0:2 * DH], ident16[:])
                for t in range(T):
                    mm = pe.transpose(bank[0:DH, N + t * P:N + (t + 1) * P], knat[:, t, 2 * DH:3 * DH], ident16[:])
                mm.then_inc(kt_ps, 1)

            def project_q(b, c, t):
                bank = claim(pe, b, f"q{c}", t)
                if c == 0 and t == 0:
                    for i in range(T):
                        drained(pe, b, "xt", i)
                rows, cols = slice(t * P, (t + 1) * P), slice(c * HC * DH, (c + 1) * HC * DH)
                products(bank[:], [(xt[:, k, rows], w[:, k, cols]) for k in range(KC)
                                   for xt, w in ((xt_hi, wq_hi), (xt_hi, wq_lo), (xt_lo, wq_hi))]).then_inc(q_ps, 1)

            def turn_q(b, p):
                c, h = p // (HC // 2), 2 * (p % (HC // 2))
                pe.wait_ge(qn_ready, at(b, 2 * T, T * c + T))
                wait(pe, qa_ready, at(b, PAIRS, p))
                for i in range(2):
                    for t in range(T):
                        mm = pe.transpose(ps_qt[:, i, t * P:(t + 1) * P], qn[c][:, t, h + i, :], ident16[:])
                mm.then_inc(qt_ps, 1)

            def scores(b, p, i):
                h, t = TILE_OF[i]
                if i == 0:
                    pe.wait_ge(qb_ready, at(b, PAIRS, p + 1))
                    pe.wait_ge(kv_ready, at(b, 1, 1))
                wait(pe, biased, at(b, 64, 8 * p + i - 1))
                o = ps_s[i % 2][:, 0:S_N[t]]
                rows = slice(t * P, (t + 1) * P)
                pe.matmul(o, qa[p % 2][:, h, rows], ka[:, 0:S_N[t]], start=True, stop=False)
                pe.matmul(o, qb[p % 2][:, h, rows], kb[0:DH + 1, 0:S_N[t]], start=False, stop=True).then_inc(qk_ps, 1)

            def turn_probs(b, p, g):
                n = GROUPS * p + g
                pe.wait_ge(normed, at(b, H, 2 * p + 1 + max(h for h, _, _ in GROUP[g])))
                wait(pe, pt_drained[n % 2], at(b, 20, n // 2))
                for h, kb_, col in GROUP[g]:
                    for t in range(kb_, T):
                        at_ = S_AT[t] + kb_ * P
                        mm = pe.transpose(ps_pt[n % 2][:, col + (t - kb_) * P:col + (t - kb_ + 1) * P],
                                          pr[:, slot(p, h), at_:at_ + P], ident[:])
                mm.then_inc(pt_ps, 1)

            def weigh_values(b, p, s):
                n = GROUPS * p + PV_NEEDS[s]
                for m in range(max(0, n - 1), n + 1):
                    pe.wait_ge(pt_drained[m % 2], at(b, 20, m // 2 + 1))
                if s == 0:
                    wait(pe, o_drained, at(b, PAIRS, p))
                    if p == 0:
                        pe.wait_ge(v_ready, at(b, 1, 1))
                for kb_, places in PV_SETS[s]:
                    for h, (g, col) in enumerate(places):
                        w = (T - kb_) * P
                        mm = pe.matmul(ps_o[h * DH:(h + 1) * DH, kb_ * P:N], v[:, kb_, :], pts[:, (GROUPS * p + g) % PSLOTS, col:col + w],
                                       start=kb_ == 0, stop=kb_ == 2)
                mm.then_inc(pv_done, 1)

            def turn_null_probs(b):
                bank = claim(pe, b, "pnt", 0)
                pe.wait_ge(pnat_ready, at(b, H, H))
                for t in range(T):
                    mm = pe.transpose(bank[0:H, t * P:(t + 1) * P], pnat[:, t, :], ident[:])
                mm.then_inc(pnt_ps, 1)

            def project_out(b, t):
                bank = claim(pe, b, "c", t)
                rows = slice(t * P, (t + 1) * P)
                if t == 0:
                    pe.wait_ge(o_drained, at(b, PAIRS, PAIRS - 1))
                    drained(pe, b, "pnt", 0)
                pe.matmul(bank[:], pnt[:, rows], nvw[:], start=True, stop=False)
                for q in range(PAIRS):
                    if t == 0 and q == PAIRS - 1:
                        pe.wait_ge(o_drained, at(b, PAIRS, PAIRS))
                    for o, w in ((ot_hi, wo_hi), (ot_hi, wo_lo), (ot_lo, wo_hi)):
                        mm = pe.matmul(bank[:], o[:, q, rows], w[:, q, :], start=False, stop=q == PAIRS - 1 and o is ot_lo)
                mm.then_inc(c_ps, 1)

            def fill(name, i, b):
                if name == "xt":
                    turn_x(b, i)
                elif name == "kv":
                    keys_values(b, "kv", kv_ps, H)
                elif name == "nul":
                    keys_values(b, "nul", nul_ps, 0)
                elif name == "kvn":
                    turn_kv(b)
                elif name == "nn":
                    turn_null(b)
                elif name in ("q0", "q1"):
                    project_q(b, int(name[1]), i)
                elif name == "pnt":
                    turn_null_probs(b)
                else:
                    project_out(b, i)

            def run(b, p):
                fb, fp = pair(b, p + 1)
                if is_lead_in(b) and p == 4:
                    pe.wait_ge(stage_read, KC + 1)
                if is_lead_in(b) and p == 5:
                    network(1)
                if is_lead_in(b) and p == 6:
                    null_value(0)
                    null_value(1)
                if is_lead_in(b) and p == 7:
                    null_value(2)
                if is_first(b) and p == 0:
                    null_value(3)
                    pe.wait_ge(weights, 1)
                for what, i in ORDER:
                    if what == "qt" and pair(b, p + 2)[0] is not None:
                        if pair(b, p + 2)[1] == 0:
                            turn_k(pair(b, p + 2)[0])
                        turn_q(*pair(b, p + 2))
                    elif what == "qk" and fb is not None:
                        scores(fb, fp, i)
                    elif what == "fill":
                        for f in fillers(b, p, i):
                            fill(*f)
                    elif what == "pt" and exists(b):
                        turn_probs(b, p, i)
                    elif what == "pv" and exists(b):
                        weigh_values(b, p, i)

            iterations(pe, run)

        @block.scalar
        def _(act):
            def hi_weights(k):
                act.wait_ge(stage_in[k % 2], 16 * (k // 2 + 1))
                if k < KC:
                    act.activation(wq_hi[:, k, :], stage[k % 2], ACT.Copy, scale=g_col[:, k:k + 1]).then_inc(hi_made, 1)
                elif k == KC:
                    act.wait_ge(wn_made, KC)
                    for j in range(KC):
                        act.activation(wkv_hi[:, j, H:], stage[0][:, j * P:(j + 1) * P], ACT.Copy, scale=g_col[:, j:j + 1])
                        a = act.activation(wkv_hi[:, j, 0:H], wn[:, j, :], ACT.Copy, scale=g_col[:, j:j + 1])
                    a.then_inc(hi_made, 1)
                else:
                    j = k - KC - 1
                    act.activation(wo_hi[:, 2 * j:2 * j + 2, :].rearrange("p a n -> p (a n)"), stage[k % 2], ACT.Copy
                                   ).then_inc(hi_made, 1)

            def sigmoids(layer):
                for m in range(T):
                    act.wait_ge(z_neg, T * layer + m + 1)
                    act.wait_ge(z_rstd, T * layer + m + 1)
                    act.activation(ez[:, m, :], z[:, m, :], ACT.Exp, scale=rstd[:, m:m + 1]).then_inc(z_exp, 1)
                act.wait_ge(z_exp, T * layer + T)
                act.activation(ez, ez, ACT.Ln, bias=1.0).then_inc(z_ln, 1)
                act.wait_ge(z_ln, layer + 1)
                for m in range(T):
                    act.activation(ez[:, m, :], ez[:, m, :], ACT.Exp, scale=-1.0).then_inc(z_sig, 1)

            def drain_turned(layer):
                for m in range(T):
                    act.wait_ge(h_turned, T * layer + m + 1)
                    act.activation(ht[:, :, m * P:(m + 1) * P],
                                   [ps_s[0], ps_s[1], ps_pt[0], ps_pt[1]][m][:, :].rearrange("p (k n) -> p k n", k=KC),
                                   ACT.Copy).then_inc(h_drained, 1)

            act.wait_ge(cols_in, 16 * 4)
            hi_weights(0)
            hi_weights(1)
            sigmoids(0)
            drain_turned(0)
            for k in range(2, KC):
                hi_weights(k)

            def fill_stage(name, i, b, s):
                if name == "xt":
                    bank, _ = bank_of(b, name, i)
                    act.wait_ge(xt_ps, at(b, T, i + 1))
                    act.activation(xt_hi[:, :, i * P:(i + 1) * P], bank[:, :].rearrange("p (k n) -> p k n", k=KC),
                                   ACT.Copy).then_inc(xt_hi_made, 1)
                elif name == "kv":
                    bank, done = bank_of(b, name, i)
                    act.wait_ge(kv_ps, at(b, 1, 1))
                    act.activation(kvt, bank[:], ACT.Copy).then_inc(done, 1)
                elif name == "nul":
                    bank, done = bank_of(b, name, i)
                    act.wait_ge(nul_ps, at(b, 1, 1))
                    act.activation(nt[:, 0:N], bank[0:H, :], ACT.Copy).then_inc(done, 1)
                elif name == "kvn":
                    bank, _ = bank_of(b, name, i)
                    act.wait_ge(kvn_ps, at(b, 1, 1))
                    act.wait_ge(qss_made, at(b, 2 * T, 1))
                    act.activation(ksq, bank[:, :].rearrange("p (t n) -> p t n", t=T)[:, :, 0:DH],
                                   ACT.Square).then_inc(ksq_made, 1)
                elif name in ("q0", "q1") and s == 1:
                    c = int(name[1])
                    drained(act, b, name, i)
                    act.activation(qn[c][:, i, :, 0:DH], qf[:], ACT.Copy).then_inc(qhi_made, 1)
                elif name in ("q0", "q1"):
                    n = at(b, 2 * T, T * int(name[1]) + i)
                    bank, _ = bank_of(b, name, i)
                    wait(act, qss_made, n)
                    if name == "q0" and i == 1:
                        act.wait_ge(kss_made, at(b, 1, 1))
                    act.wait_ge(q_ps, n + 1)
                    act.activation(qsq[:], bank[:, :].rearrange("p (h d) -> p h d", h=HC), ACT.Square).then_inc(qsq_made, 1)
                elif name == "pnt":
                    bank, _ = bank_of(b, name, i)
                    act.wait_ge(pnt_ps, at(b, 1, 1))
                    act.activation(pnt[0:H, :], bank[0:H, :], ACT.Copy)
                    act.activation(pnt[Q:Q + H, :], bank[0:H, :], ACT.Copy).then_inc(pnh_made, 1)

            def run(b, p):
                fb, fp = pair(b, p + 1)
                if is_lead_in(b) and p == 4:
                    hi_weights(KC)
                    sigmoids(1)
                if is_lead_in(b) and p == 5:
                    drain_turned(1)
                if is_lead_in(b) and p == 6:
                    hi_weights(KC + 1)
                    hi_weights(KC + 2)
                if is_lead_in(b) and p == 7:
                    hi_weights(KC + 3)
                if is_first(b) and p == 0:
                    hi_weights(KC + 4)
                    act.wait_ge(nvw_acc, PAIRS // 2)
                    act.wait_ge(zeros, 2)
                    act.activation(nvw[0:H, :], ps_o[0:H, :], ACT.Copy)
                    act.activation(nvw[2 * Q:2 * Q + H, :], ps_o[0:H, :], ACT.Copy).then_inc(nvw_hi_made, 1)
                for step, (what, i) in enumerate(ORDER):
                    if what == "qk" and fb is not None:
                        h, t = TILE_OF[i]
                        s = slot(fp, h)
                        act.wait_ge(biased, at(fb, 64, 8 * fp + i + 1))
                        if i % T == 0:
                            wait(act, den_ready, at(fb, H, 2 * fp + h - HEADSLOTS + 1))
                        e = pr[:, s, S_AT[t]:S_AT[t] + S_N[t]]
                        act.activation(e, e, ACT.Exp, bias=mn[:, s, t:t + 1], scale=-1.0,
                                       accum_out=rs[:, s, t:t + 1]).then_inc(exp_done, 1)
                    if step in PTS_AT and exists(b):
                        for g in range(GROUPS):
                            if PTS_AT[g] == step and g not in PT_BY_DVE:
                                drain_group(act, b, p, g)
                    if step == OH_AT and exists(b):
                        act.wait_ge(pv_done, at(b, 3 * PAIRS, 3 * p + 3))
                        if p == 0:
                            wait(act, c_ps, at(b, T, 0))
                        act.activation(ot_hi[:, p, :], ps_o[:], ACT.Copy).then_inc(oh_made, 1)
                    for f in stages(ACT_STAGES, b, p, step):
                        fill_stage(*f)
                    if step in PN_AT and fb is not None:
                        h = PN_AT.index(step)
                        s = slot(fp, h)
                        act.wait_ge(dn_ready, at(fb, H, 2 * fp + h + 1))
                        act.activation(pn[:, s, :], dn[:, s, :], ACT.Exp, scale=-1.0).then_inc(pn_ready, 1)

            def drain_group(act, b, p, g):
                n = GROUPS * p + g
                act.wait_ge(pt_ps, at(b, GROUPS * PAIRS, n + 1))
                wait(act, pv_done, at(b, 3 * PAIRS, slot_free(n)))
                act.activation(pts[:, n % PSLOTS, :], ps_pt[n % 2][:], ACT.Copy).then_inc(pt_drained[n % 2], 1)

            iterations(act, run)

        @block.gpsimd
        def _(pool):
            pool.memset(ident[:], 0.0).then_inc(id_zero, 1)
            pool.memset(half[:], -0.5).then_inc(consts, 1)
            pool.memset(eps[:], EPS).then_inc(consts, 1)
            pool.memset(nv_blk, 0.0).then_inc(consts, 1)
            pool.iota(dist[:], pattern=[[-P, T]], base=N - 1, channel_multiplier=-1,
                      allow_small_or_imprecise_dtypes=True).then_inc(consts, 1)
            pool.wait_ge(id_zero, 1)
            pool.affine_select(out=ident[:], in_=ident[:], compare_op=ALU.not_equal, fill=1.0, base=0,
                               pattern=[[-1, P]], channel_multiplier=1).then_inc(id_made, 1)
            pool.wait_ge(consts, 4)

            def root(dst, src, width, ready):
                pool.tensor_tensor(dst, src, half[:, 0:width], ALU.pow).then_inc(ready, 1)

            def rstd_of_network(layer):
                for m in range(T):
                    pool.wait_ge(z_mv, T * layer + m + 1)
                    pool.tensor_tensor(ve[:, m:m + 1], mv[:, m, 1:2], eps[:, 0:1], ALU.add).then_inc(z_ve, 1)
                    pool.wait_ge(z_ve, T * layer + m + 1)
                    root(rstd[:, m:m + 1], ve[:, m:m + 1], 1, z_rstd)

            rstd_of_network(0)
            pool.wait_ge(vec, 3)
            root(nk_ss[:, 2:3], nk_ss[:, 1:2], 1, nk_pow)
            for k in range(KC):
                pool.wait_ge(vec, 4)
                pool.wait_ge(stage_in[k % 2], 16 * (k // 2 + 1))
                wait(pool, wn_made, k)
                pool.tensor_tensor(prod.rearrange("p (h d) -> p h d", h=H), stage[k % 2].rearrange("p (h d) -> p h d", h=H),
                                   nk_row[:].unsqueeze(1).broadcast_to([P, H, DH]), ALU.mult).then_inc(prod_made, 1)

            def fill_stage(name, i, b, s):
                if name == "xt":
                    pool.wait_ge(mv_ready, at(b, T, i + 1))
                    pool.tensor_tensor(ve[:, i:i + 1], mv[:, i, 1:2], eps[:, 0:1], ALU.add).then_inc(ve_made, 1)
                    pool.wait_ge(ve_made, at(b, T, i + 1))
                    root(rstd[:, i:i + 1], ve[:, i:i + 1], 1, rstd_ready)
                elif name == "kvn":
                    pool.wait_ge(kssg_made, at(b, 1, 1))
                    root(rk[:], kssg[:], T, rk_ready)
                elif name in ("q0", "q1"):
                    c = int(name[1])
                    n = at(b, 2 * T, T * c + i)
                    if s == 0:
                        pool.wait_ge(qssg_made, n + 1)
                        root(rq[:, i % 2, :], qssg[:, i % 2, :], HC, rq_ready)
                        return
                    if c == 0 and i == 0:
                        drained(pool, b, "nn", 0)
                    pool.wait_ge(rq_ready, n + 1)
                    pool.tensor_tensor(nsq[:], nsr[:, i, c * HC:(c + 1) * HC], rq[:, i % 2, :], ALU.mult).then_inc(nsq_made, 1)
                    pool.wait_ge(nsq_made, n + 1)
                    pool.tensor_tensor(nsn[:, i, c * HC:(c + 1) * HC], nsq[:], nb_row[:, c * HC:(c + 1) * HC],
                                       ALU.subtract).then_inc(nsn_ready, 1)
                elif name == "c":
                    pool.wait_ge(cmv_ready, at(b, T, i + 1))
                    pool.tensor_tensor(cve[:, i % 2, :], cmv[:, i % 2, 1:2], eps[:, 0:1], ALU.add).then_inc(cve_made, 1)
                    pool.wait_ge(cve_made, at(b, T, i + 1))
                    root(crs[:, i % 2, :], cve[:, i % 2, :], 1, crs_ready)

            def null_score(b, p, h):
                s = slot(p, h)
                pool.wait_ge(biased, at(b, 64, 8 * p + T * (h + 1)))
                pool.tensor_tensor(dn[:, s, :], nsn[:, :, 2 * p + h], mn[:, s, :], ALU.subtract).then_inc(dn_ready, 1)

            def denominator(b, p, h):
                s = slot(p, h)
                pool.wait_ge(pn_ready, at(b, H, 2 * p + h + 1))
                pool.tensor_tensor(den[:, s, :], rs[:, s, :], pn[:, s, :], ALU.add).then_inc(den_ready, 1)

            def normalise(b, p, h):
                s = slot(p, h)
                pool.wait_ge(rr_ready, at(b, H, 2 * p + h + 1))
                if p == 0 and h == 0:
                    wait(pool, pnt_ps, at(b, 1, 0))
                pool.tensor_tensor(pnat[:, :, 2 * p + h], pn[:, s, :], rr[:, s, :], ALU.mult).then_inc(pnat_ready, 1)
                for t in range(T):
                    e = pr[:, s, S_AT[t]:S_AT[t] + S_N[t]]
                    m = pool.tensor_tensor(e, e, rr[:, s, t:t + 1].broadcast_to([P, S_N[t]]), ALU.mult)
                m.then_inc(normed, 1)

            def run(b, p):
                fb, fp = pair(b, p + 1)
                if is_lead_in(b) and p == 4:
                    rstd_of_network(1)
                for step in range(STEPS):
                    if step in DN_AT and fb is not None:
                        null_score(fb, fp, DN_AT.index(step))
                    if step in DEN_AT and fb is not None:
                        denominator(fb, fp, DEN_AT.index(step))
                    for f in stages(POOL_STAGES, b, p, step):
                        fill_stage(*f)
                    if step in NORM_AT and fb is not None:
                        normalise(fb, fp, NORM_AT.index(step))

            iterations(pool, run)

        @block.vector
        def _(dve):
            dve.wait_ge(id_made, 1)
            dve.tensor_copy(ident16[:], ident[:]).then_inc(id_made, 1)
            for i in range(2):
                dve.memset(qb[i][DH:DH + 1], PADK)
            dve.memset(nvw[:].bitcast(F32), 0.0).then_inc(zeros, 1)
            dve.memset(pnt[:].bitcast(F32), 0.0).then_inc(zeros, 1)
            dve.wait_ge(net_in, 16 * 3)
            dve.wait_ge(consts, 4)
            dve.tensor_scalar(row_g0, row_g0, -1.0, None, ALU.mult).then_inc(gains, 1)

            def null_key():
                dve.wait_ge(cols_in, 16 * 4)
                dve.scalar_tensor_tensor(s_row[:], s_row[:], -SCALE, ks_row[:], ALU.mult, ALU.mult).then_inc(vec, 1)
                dve.tensor_tensor_reduce(nk_sq, nk_row[:], nk_row[:], 1.0, 0.0, ALU.mult, ALU.add, nk_ss[:, 0:1]).then_inc(vec, 1)
                dve.wait_ge(vec, 2)
                dve.tensor_scalar(nk_ss[:, 1:2], nk_ss[:, 0:1], 1e-24, None, ALU.max).then_inc(vec, 1)
                dve.wait_ge(nk_pow, 1)
                dve.scalar_tensor_tensor(nk_row[:], nk_row[:], nk_ss[:, 2:3], s_row[:], ALU.mult, ALU.mult).then_inc(vec, 1)

            def null_value():
                dve.wait_ge(rows_in, ROWS_IN)
                dve.tensor_scalar(row_g1, row_g1, -1.0, None, ALU.mult).then_inc(gains, 1)
                for h in range(2):
                    dst = nv_blk[h * DH:(h + 1) * DH, :, :].rearrange("p a b -> p (a b)")[:, h:h + (H + 2) * (PAIRS - 1) + 1:H + 2]
                    dve.tensor_copy(dst, nv_col[h * DH:(h + 1) * DH, :].broadcast_to([DH, PAIRS])).then_inc(vec, 1)
                dve.memset(kb[:], 0.0).then_inc(vec, 1)
                dve.wait_ge(vec, 7)

            def lo_weights(k):
                f = stage[k % 2]
                dve.wait_ge(hi_made, k + 1)
                if k < KC:
                    dve.scalar_tensor_tensor(wq_lo[:, k, :], f, g_col[:, k:k + 1], wq_hi[:, k, :].bitcast(F32),
                                             ALU.mult, ALU.subtract).then_inc(stage_read, 1)
                    dve.wait_ge(prod_made, k + 1)
                    dve.tensor_reduce(wn[:, k, :], prod.rearrange("p (h d) -> p h d", h=H), AX.X, ALU.add).then_inc(wn_made, 1)
                elif k == KC:
                    for j in range(KC):
                        dve.scalar_tensor_tensor(wkv_lo[:, j, 0:H], wn[:, j, :], g_col[:, j:j + 1],
                                                 wkv_hi[:, j, 0:H].bitcast(F32), ALU.mult, ALU.subtract)
                        a = dve.scalar_tensor_tensor(wkv_lo[:, j, H:], f[:, j * P:(j + 1) * P], g_col[:, j:j + 1],
                                                     wkv_hi[:, j, H:].bitcast(F32), ALU.mult, ALU.subtract)
                    a.then_inc(stage_read, 1)
                else:
                    j = k - KC - 1
                    dst = wo_lo[:, 2 * j:2 * j + 2, :].rearrange("p a n -> p (a n)")
                    hi = wo_hi[:, 2 * j:2 * j + 2, :].rearrange("p a n -> p (a n)").bitcast(F32)
                    dve.tensor_tensor(dst, f, hi, ALU.subtract).then_inc(stage_read, 1)

            def layernorm(layer):
                for m in range(T):
                    if layer == 0:
                        dve.scalar_tensor_tensor(z[:, m, :], row_w0, dist[:, m:m + 1], row_b0, ALU.mult, ALU.add).then_inc(z_sum, 1)
                    else:
                        dve.wait_ge(h_mm, m + 1)
                        bank = [ps_s[0], ps_s[1], ps_pt[0], ps_pt[1]][m]
                        dve.tensor_tensor(z[:, m, :], row_b1, bank[:], ALU.subtract).then_inc(z_sum, 1)
                    dve.wait_ge(z_sum, T * layer + m + 1)
                    dve.bn_stats(bn6[:, m, :], z[:, m, :]).then_inc(z_stats, 1)
                    dve.wait_ge(z_stats, T * layer + m + 1)
                    dve.bn_aggr(mv[:, m, :], bn6[:, m, :]).then_inc(z_mv, 1)
                    dve.wait_ge(z_mv, T * layer + m + 1)
                    dve.wait_ge(gains, layer + 1)
                    dve.scalar_tensor_tensor(z[:, m, :], z[:, m, :], mv[:, m, 0:1], (row_g0, row_g1)[layer], ALU.subtract, ALU.mult
                                             ).then_inc(z_neg, 1)

            def activations(layer):
                for m in range(T):
                    dve.wait_ge(z_sig, T * layer + m + 1)
                    dve.scalar_tensor_tensor(z[:, m, :], z[:, m, :], rstd[:, m:m + 1], ez[:, m, :], ALU.mult, ALU.mult
                                             ).then_inc(z_act, 1)

            def finish_table():
                dve.wait_ge(z_act, 2 * T)
                dve.memset(tab[:, N:RW], MASKED).then_inc(tab_made, 1)
                dve.wait_ge(tab_ps, 1)
                dve.tensor_scalar(tab[:, 0:N], ps_o[0:H, :], b2_col[:], None, ALU.subtract).then_inc(tab_made, 1)

            layernorm(0)
            null_key()
            lo_weights(0)
            lo_weights(1)
            activations(0)
            null_value()
            for k in range(2, KC):
                lo_weights(k)

            def rows_of_x(b, t, s):
                bank, done = bank_of(b, "xt", t)
                if s == 0:
                    dve.wait_ge(x_in[t % 2], at(b, 32, 16 * (t // 2 + 1)))
                    dve.bn_stats(bn6[:, t, :], xs[:, t % 2, :]).then_inc(stats, 1)
                    wait_apart(stats, at(b, T, t + 1))
                    dve.bn_aggr(mv[:, t, :], bn6[:, t, :]).then_inc(mv_ready, 1)
                elif s == 1:
                    dve.wait_ge(rstd_ready, at(b, T, t + 1))
                    dve.tensor_scalar(xs[:, t % 2, :], xs[:, t % 2, :], mv[:, t, 0:1], rstd[:, t:t + 1], ALU.subtract, ALU.mult
                                      ).then_inc(xn_ready, 1)
                else:
                    dve.wait_ge(xt_hi_made, at(b, T, t + 1))
                    dst, hi = (a[:, :, t * P:(t + 1) * P] for a in (xt_lo, xt_hi))
                    dve.tensor_tensor(dst, bank[:, :].rearrange("p (k n) -> p k n", k=KC), hi.bitcast(F32),
                                      ALU.subtract).then_inc(done, 1)

            def keys(b, s):
                bank, done = bank_of(b, "kvn", 0)
                rows = bank[:, :].rearrange("p (t n) -> p t n", t=T)
                if s == 0:
                    dve.wait_ge(ksq_made, at(b, 1, 1))
                    dve.tensor_reduce(kss[:], ksq, AX.X, ALU.add).then_inc(kss_made, 1)
                    dve.tensor_copy(vst[:], rows[:, :, DH:]).then_inc(vst_made, 1)
                    dve.wait_ge(kss_made, at(b, 1, 1))
                    dve.tensor_scalar(kssg[:], kss[:], 1e-24, None, ALU.max).then_inc(kssg_made, 1)
                    return
                dve.wait_ge(qn_ready, at(b, 2 * T, 1))
                dve.wait_ge(rk_ready, at(b, 1, 1))
                for t in range(T):
                    a = dve.scalar_tensor_tensor(kh[:, t, :], rows[:, t, 0:DH], rk[:, t:t + 1], s_row[:], ALU.mult, ALU.mult)
                a.then_inc(done, 1)
                drained(dve, b, "kvn", 0)
                wait(dve, kt_ps, at(b, 1, 0))
                hi = knat[:, :, 0:2 * DH].rearrange("p t (a d) -> p t a d", a=2)
                dve.tensor_copy(hi, kh.unsqueeze(2).broadcast_to([P, T, 2, DH])).then_inc(khi_made, 1)
                dve.wait_ge(khi_made, at(b, 1, 1))
                dve.tensor_tensor(knat[:, :, 2 * DH:], kh, knat[:, :, 0:DH], ALU.subtract).then_inc(kn_ready, 1)

            def settle_kv(b):
                bank, done = bank_of(b, "kt", 0)
                f16 = bank[:, :].bitcast(F16)
                dve.wait_ge(kt_ps, at(b, 1, 1))
                dve.tensor_copy(ka[:], f16[:, 0:N])
                dve.tensor_copy(kb[0:DH, :], f16[0:DH, N:]).then_inc(done, 1)
                dve.wait_ge(mask_in, at(b, 16, 16))
                dve.tensor_scalar(kb[DH:DH + 1, :], mask_u8[DH:DH + 1, :], -PADK, PADK, ALU.mult, ALU.add).then_inc(kv_ready, 1)

            def settle_v(b):
                wait(dve, pv_done, at(b, 3 * PAIRS, 0))
                dve.wait_ge(vst_made, at(b, 1, 1))
                dve.tensor_copy(v[:], vst[:]).then_inc(v_ready, 1)

            def split_q(b, c, i, s):
                n = at(b, 2 * T, T * c + i)
                bank, done = bank_of(b, f"q{c}", i)
                if s == 0:
                    dve.wait_ge(qsq_made, n + 1)
                    dve.tensor_reduce(qss[:], qsq[:], AX.X, ALU.add).then_inc(qss_made, 1)
                    dve.wait_ge(qss_made, n + 1)
                    wait(dve, rq_ready, n - 1)
                    dve.tensor_scalar(qssg[:, i % 2, :], qss[:], 1e-24, None, ALU.max).then_inc(qssg_made, 1)
                    return
                if c == 0 and i == 1:
                    dve.wait_ge(kn_ready, at(b, 1, 1))
                else:
                    wait(dve, qn_ready, n)
                dve.wait_ge(rq_ready, n + 1)
                dve.tensor_tensor(qf[:], bank[:, :].rearrange("p (h d) -> p h d", h=HC),
                                  rq[:, i % 2, :].unsqueeze(2).broadcast_to([P, HC, DH]), ALU.mult).then_inc(done, 1)

            def low_q(b, c, i):
                n = at(b, 2 * T, T * c + i)
                dve.wait_ge(qhi_made, n + 1)
                dve.tensor_tensor(qn[c][:, i, :, DH:], qf[:], qn[c][:, i, :, 0:DH], ALU.subtract).then_inc(qn_ready, 1)

            def finish_rows(b, t, s):
                bank, done = bank_of(b, "c", t)
                if s == 0:
                    dve.wait_ge(c_ps, at(b, T, t + 1))
                    dve.bn_stats(cbn6[:], bank[:]).then_inc(cstats, 1)
                    wait_apart(cstats, at(b, T, t + 1))
                    dve.bn_aggr(cmv[:, t % 2, :], cbn6[:]).then_inc(cmv_ready, 1)
                    dve.wait_ge(cmv_ready, at(b, T, t + 1))
                    dve.scalar_tensor_tensor(bank[:], bank[:], cmv[:, t % 2, 0:1], gout_row[:], ALU.subtract, ALU.mult
                                             ).then_inc(og_made, 1)
                    return
                dve.wait_ge(og_made, at(b, T, t + 1))
                dve.wait_ge(crs_ready, at(b, T, t + 1))
                dve.wait_ge(res_in[t % 2], at(b, 16 * (T // 2), 16 * (t // 2 + 1)))
                dve.scalar_tensor_tensor(res[t % 2][:], bank[:], crs[:, t % 2, :], res[t % 2][:], ALU.mult, ALU.add).then_inc(done, 1)

            def fill_stage(name, i, b, s):
                bank, done = bank_of(b, name, i)
                if name == "xt":
                    rows_of_x(b, i, s)
                elif name == "kvn":
                    keys(b, s)
                elif name == "nn":
                    dve.wait_ge(nn_ps, at(b, 1, 1))
                    wait(dve, nsn_ready, at(b, 2 * T, 0))
                    dve.tensor_copy(nsr[:], bank[:, 0:T * H].rearrange("p (t h) -> p t h", t=T)).then_inc(done, 1)
                elif name in ("q0", "q1"):
                    if s < 2:
                        split_q(b, int(name[1]), i, s)
                    else:
                        low_q(b, int(name[1]), i)
                elif name == "pnt":
                    dve.wait_ge(pnh_made, at(b, 1, 1))
                    dve.tensor_tensor(pnt[2 * Q:2 * Q + H, :], bank[0:H, :], pnt[0:H, :].bitcast(F32), ALU.subtract).then_inc(done, 1)
                elif name == "c":
                    finish_rows(b, i, s)

            def add_bias(b, p, i):
                h, t = TILE_OF[i]
                s = slot(p, h)
                if i == 0:
                    dve.wait_ge(tb_in[p % 2], at(b, 16 * PAIRS // 2, 16 * (p // 2 + 1)))
                    dve.wait_ge(nsn_ready, at(b, 2 * T, T * (p // (HC // 2)) + T))
                    wait(dve, pt_ps, at(b, GROUPS * PAIRS, GROUPS * (p - 1)))
                    wait(dve, dn_ready, at(b, H, 2 * p - 2))
                wait_apart(qk_ps, at(b, 64, 8 * p + i + 1))
                off = (T - 1 - t) * P
                dve.tensor_tensor_reduce(pr[:, s, S_AT[t]:S_AT[t] + S_N[t]], ps_s[i % 2][:, 0:S_N[t]],
                                         tb[p % 2][:, h, off:off + S_N[t]], 1.0, nsn[:, t, 2 * p + h:2 * p + h + 1],
                                         ALU.add, ALU.min, mn[:, s, t:t + 1]).then_inc(biased, 1)

            def invert(b, p, h):
                s = slot(p, h)
                dve.wait_ge(den_ready, at(b, H, 2 * p + h + 1))
                dve.reciprocal(rr[:, s, :], den[:, s, :]).then_inc(rr_ready, 1)

            def run(b, p):
                fb, fp = pair(b, p + 1)
                if is_lead_in(b) and p == 4:
                    layernorm(1)
                    lo_weights(KC)
                    activations(1)
                if is_lead_in(b) and p == 5:
                    finish_table()
                if is_lead_in(b) and p == 6:
                    lo_weights(KC + 1)
                    lo_weights(KC + 2)
                if is_lead_in(b) and p == 7:
                    lo_weights(KC + 3)
                if is_first(b) and p == 0:
                    lo_weights(KC + 4)
                    dve.wait_ge(nvw_hi_made, 1)
                    dve.tensor_tensor(nvw[Q:Q + H, :], ps_o[0:H, :], nvw[0:H, :].bitcast(F32), ALU.subtract).then_inc(weights, 1)
                for step, (what, i) in enumerate(ORDER):
                    if what == "qk" and fb is not None:
                        add_bias(fb, fp, i)
                    if step == QA_AT and pair(b, p + 2)[0] is not None:
                        qb_, qp = pair(b, p + 2)
                        if qp == 0:
                            settle_kv(qb_)
                        dve.wait_ge(qt_ps, at(qb_, PAIRS, qp + 1))
                        dve.tensor_copy(qa[qp % 2][:], ps_qt[:]).then_inc(qa_ready, 1)
                    if step == QB_AT and pair(b, p + 2)[0] is not None:
                        qb_, qp = pair(b, p + 2)
                        dve.wait_ge(qa_ready, at(qb_, PAIRS, qp + 1))
                        dve.tensor_copy(qb[qp % 2][0:DH], qa[qp % 2][0:DH]).then_inc(qb_ready, 1)
                    for g in PT_BY_DVE:
                        if PTS_AT[g] == step and exists(b):
                            n = GROUPS * p + g
                            dve.wait_ge(pt_ps, at(b, GROUPS * PAIRS, n + 1))
                            wait(dve, pv_done, at(b, 3 * PAIRS, slot_free(n)))
                            dve.tensor_copy(pts[:, n % PSLOTS, :], ps_pt[n % 2][:]).then_inc(pt_drained[n % 2], 1)
                    if step == OL_AT and exists(b):
                        dve.wait_ge(oh_made, at(b, PAIRS, p + 1))
                        dve.tensor_tensor(ot_lo[:, p, :], ps_o[:], ot_hi[:, p, :].bitcast(F32), ALU.subtract).then_inc(o_drained, 1)
                    for f in stages(DVE_STAGES, b, p, step):
                        fill_stage(*f)
                    if step in RR_AT and fb is not None:
                        invert(fb, fp, RR_AT.index(step))
                if p == PAIRS - 1 and fb is not None:
                    settle_v(fb)

            iterations(dve, run)


ROWS_IN = 16 * 8
_INS = ["x", "cond_64", "mask_BxS_bf1", "L0_cond_g_norm", "L0_cond_Wq", "L0_cond_Wkv", "L0_cond_q_scale",
        "L0_cond_k_scale", "L0_cond_null_attn_bias", "L0_cond_w0", "L0_cond_b0", "L0_cond_g0", "L0_cond_w1",
        "L0_cond_b1", "L0_cond_g1", "L0_cond_w2", "L0_cond_b2", "L0_cond_Wout", "L0_cond_g_out"]


def kernel(**inputs):
    import numpy as _np
    import concourse.bacc as _bacc
    from concourse import mybir as _mybir
    from concourse.bass_utils import run_bass_kernel_spmd as _run

    nc = _bacc.Bacc("TRN2", target_bir_lowering=False, num_devices=1)
    arrays, args = {}, []
    for name in _INS:
        a = _np.ascontiguousarray(inputs[name])
        if a.dtype == _np.bool_:
            a = a.view(_np.uint8)
        arrays[name] = a
        args.append(nc.dram_tensor(name, a.shape, _mybir.dt.from_np(a.dtype), kind="ExternalInput").ap())
    out = nc.dram_tensor("out", (B, N, D), _mybir.dt.float32, kind="ExternalOutput").ap()
    build(nc, *args, out)
    r = _run(nc, [arrays], core_ids=[0])
    return r.results[0]["out"]
```
